# Optimizing a Trainium2 kernel written in Bass

```python
import numpy as np
import jax
import jax.numpy as jnp

def _softmax(x, axis=-1):
    return jax.nn.softmax(x, axis=axis)

def _gelu(x):
    return jax.nn.gelu(x, approximate=True)

def _silu(x):
    return jax.nn.silu(x)

def _sigmoid(x):
    return jax.nn.sigmoid(x)

def _layernorm(x, axis=-1, eps=1e-05):
    m = jnp.mean(x, axis=axis, keepdims=True)
    v = jnp.var(x, axis=axis, keepdims=True)
    return (x - m) / jnp.sqrt(v + eps)

def _scatter_add(tgt, idx, src, axis=0):
    return tgt.at[idx].add(src)

def _segment_sum(src, seg, n):
    return jax.ops.segment_sum(src, seg, n)
kernel_name = 'mk_hybrid_d1_jaxref_r8_ac3e63'

def setup_inputs(seed: int=0):
    np.random.seed(seed)
    _w = jnp.asarray

    def _L0_attn_a_setup():
        import jax, jax.numpy as jnp
        import numpy as np
        D_MODEL = 128
        N_HEADS = 16
        HEAD_DIM = D_MODEL // N_HEADS
        SCALE = HEAD_DIM ** (-0.5)

        def apply_rotary(x):
            seq_len = x.shape[-2]
            freqs = 10000.0 ** (jnp.arange(0, HEAD_DIM, 2.0, dtype=jnp.float32) / HEAD_DIM)
            t = jnp.arange(seq_len, dtype=jnp.float32)
            angles = t[:, None] * freqs[None, :]
            sin = jnp.sin(angles)[None, None]
            cos = jnp.cos(angles)[None, None]
            x1, x2 = (x[..., ::2], x[..., 1::2])
            return jnp.concatenate([x1 * cos - x2 * sin, x2 * cos + x1 * sin], axis=-1)
        key = jax.random.key(seed)
        ks = jax.random.split(key, 5)
        B, T = (2, 256)
        std = D_MODEL ** (-0.5)
        return {'x': jax.random.normal(ks[0], (B, T, D_MODEL), dtype=jnp.float32), 'qkv_w': jax.random.normal(ks[1], (D_MODEL, 3 * D_MODEL), dtype=jnp.float32) * std, 'qkv_b': jnp.zeros((3 * D_MODEL,), dtype=jnp.float32), 'out_w': jax.random.normal(ks[2], (D_MODEL, D_MODEL), dtype=jnp.float32) * std, 'out_b': jnp.zeros((D_MODEL,), dtype=jnp.float32)}
    _L0_attn_a_in = _L0_attn_a_setup()

    def _L0_attn_b_setup():
        import jax, jax.numpy as jnp
        import numpy as np
        D_MODEL = 128
        N_HEADS = 16
        HEAD_DIM = D_MODEL // N_HEADS
        SCALE = HEAD_DIM ** (-0.5)

        def apply_rotary(x):
            seq_len = x.shape[-2]
            freqs = 10000.0 ** (jnp.arange(0, HEAD_DIM, 2.0, dtype=jnp.float32) / HEAD_DIM)
            t = jnp.arange(seq_len, dtype=jnp.float32)
            angles = t[:, None] * freqs[None, :]
            sin = jnp.sin(angles)[None, None]
            cos = jnp.cos(angles)[None, None]
            x1, x2 = (x[..., ::2], x[..., 1::2])
            return jnp.concatenate([x1 * cos - x2 * sin, x2 * cos + x1 * sin], axis=-1)
        key = jax.random.key(seed)
        ks = jax.random.split(key, 5)
        B, T = (2, 256)
        std = D_MODEL ** (-0.5)
        return {'x': jax.random.normal(ks[0], (B, T, D_MODEL), dtype=jnp.float32), 'qkv_w': jax.random.normal(ks[1], (D_MODEL, 3 * D_MODEL), dtype=jnp.float32) * std, 'qkv_b': jnp.zeros((3 * D_MODEL,), dtype=jnp.float32), 'out_w': jax.random.normal(ks[2], (D_MODEL, D_MODEL), dtype=jnp.float32) * std, 'out_b': jnp.zeros((D_MODEL,), dtype=jnp.float32)}
    _L0_attn_b_in = _L0_attn_b_setup()

    def _L0_ffn_setup():
        import jax, jax.numpy as jnp
        import numpy as np
        B, S, H, F, G = (8, 256, 128, 512, 128)
        EPS = 1e-05

        def _dequant(q, scales, g):
            K, N = q.shape
            w = (q.astype(jnp.float32) - 128.0).reshape(K // g, g, N) * scales[:, None, :]
            return w.reshape(K, N)
        key = jax.random.key(seed)
        ks = jax.random.split(key, 8)
        x = jax.random.normal(ks[0], (B, S, H), dtype=jnp.float32)
        ln_gamma = jnp.ones((H,), jnp.float32)
        ln_beta = jnp.zeros((H,), jnp.float32)
        fc1_q = jax.random.randint(ks[1], (H, F), 0, 32, dtype=jnp.int32)
        fc2_q = jax.random.randint(ks[2], (F, H), 0, 32, dtype=jnp.int32)
        fc1_scales = jax.random.uniform(ks[3], (H // G, F), jnp.float32) * 0.02 + 0.001
        fc2_scales = jax.random.uniform(ks[4], (F // G, H), jnp.float32) * 0.02 + 0.001
        fc1_bias = jax.random.normal(ks[5], (F,), jnp.float32) * 0.02
        fc2_bias = jax.random.normal(ks[6], (H,), jnp.float32) * 0.02
        return {'x': x, 'ln_gamma': ln_gamma, 'ln_beta': ln_beta, 'fc1_q': fc1_q, 'fc1_scales': fc1_scales, 'fc1_bias': fc1_bias, 'fc2_q': fc2_q, 'fc2_scales': fc2_scales, 'fc2_bias': fc2_bias}
    _L0_ffn_in = _L0_ffn_setup()
    _d = {'L0_attn_a_x': _L0_attn_a_in['x'], 'L0_attn_a_qkv_w': _L0_attn_a_in['qkv_w'], 'L0_attn_a_qkv_b': _L0_attn_a_in['qkv_b'], 'L0_attn_a_out_w': _L0_attn_a_in['out_w'], 'L0_attn_a_out_b': _L0_attn_a_in['out_b'], 'L0_attn_b_qkv_w': _L0_attn_b_in['qkv_w'], 'L0_attn_b_qkv_b': _L0_attn_b_in['qkv_b'], 'L0_attn_b_out_w': _L0_attn_b_in['out_w'], 'L0_attn_b_out_b': _L0_attn_b_in['out_b'], 'L0_ffn_ln_gamma': _L0_ffn_in['ln_gamma'], 'L0_ffn_ln_beta': _L0_ffn_in['ln_beta'], 'L0_ffn_fc1_q': _L0_ffn_in['fc1_q'], 'L0_ffn_fc1_scales': _L0_ffn_in['fc1_scales'], 'L0_ffn_fc1_bias': _L0_ffn_in['fc1_bias'], 'L0_ffn_fc2_q': _L0_ffn_in['fc2_q'], 'L0_ffn_fc2_scales': _L0_ffn_in['fc2_scales'], 'L0_ffn_fc2_bias': _L0_ffn_in['fc2_bias']}
    _x0 = _d['L0_attn_a_x']
    _d['L0_attn_a_x'] = jax.random.normal(jax.random.fold_in(jax.random.key(seed), 1), (16, 512, 128), dtype=_x0.dtype)
    del _x0
    return _d

def reference(L0_attn_a_x, L0_attn_a_qkv_w, L0_attn_a_qkv_b, L0_attn_a_out_w, L0_attn_a_out_b, L0_attn_b_qkv_w, L0_attn_b_qkv_b, L0_attn_b_out_w, L0_attn_b_out_b, L0_ffn_ln_gamma, L0_ffn_ln_beta, L0_ffn_fc1_q, L0_ffn_fc1_scales, L0_ffn_fc1_bias, L0_ffn_fc2_q, L0_ffn_fc2_scales, L0_ffn_fc2_bias):

    def _L0_attn_a_ref(x, qkv_w, qkv_b, out_w, out_b):
        import jax, jax.numpy as jnp
        import numpy as np
        D_MODEL = 128
        N_HEADS = 16
        HEAD_DIM = D_MODEL // N_HEADS
        SCALE = HEAD_DIM ** (-0.5)

        def apply_rotary(x):
            seq_len = x.shape[-2]
            freqs = 10000.0 ** (jnp.arange(0, HEAD_DIM, 2.0, dtype=jnp.float32) / HEAD_DIM)
            t = jnp.arange(seq_len, dtype=jnp.float32)
            angles = t[:, None] * freqs[None, :]
            sin = jnp.sin(angles)[None, None]
            cos = jnp.cos(angles)[None, None]
            x1, x2 = (x[..., ::2], x[..., 1::2])
            return jnp.concatenate([x1 * cos - x2 * sin, x2 * cos + x1 * sin], axis=-1)
        B, T, D = x.shape
        qkv = x @ qkv_w + qkv_b
        q, k, v = jnp.split(qkv, 3, axis=-1)

        def to_heads(a):
            return a.reshape(B, T, N_HEADS, HEAD_DIM).transpose(0, 2, 1, 3)
        q, k, v = (to_heads(q), to_heads(k), to_heads(v))
        q = apply_rotary(q)
        k = apply_rotary(k)
        scores = jnp.einsum('bhqd,bhkd->bhqk', q, k) * SCALE
        weights = jax.nn.softmax(scores, axis=-1)
        attn = jnp.einsum('bhqk,bhkd->bhqd', weights, v)
        attn = attn.transpose(0, 2, 1, 3).reshape(B, T, D)
        return attn @ out_w + out_b

    def _L0_attn_b_ref(x, qkv_w, qkv_b, out_w, out_b):
        import jax, jax.numpy as jnp
        import numpy as np
        D_MODEL = 128
        N_HEADS = 16
        HEAD_DIM = D_MODEL // N_HEADS
        SCALE = HEAD_DIM ** (-0.5)

        def apply_rotary(x):
            seq_len = x.shape[-2]
            freqs = 10000.0 ** (jnp.arange(0, HEAD_DIM, 2.0, dtype=jnp.float32) / HEAD_DIM)
            t = jnp.arange(seq_len, dtype=jnp.float32)
            angles = t[:, None] * freqs[None, :]
            sin = jnp.sin(angles)[None, None]
            cos = jnp.cos(angles)[None, None]
            x1, x2 = (x[..., ::2], x[..., 1::2])
            return jnp.concatenate([x1 * cos - x2 * sin, x2 * cos + x1 * sin], axis=-1)
        B, T, D = x.shape
        qkv = x @ qkv_w + qkv_b
        q, k, v = jnp.split(qkv, 3, axis=-1)

        def to_heads(a):
            return a.reshape(B, T, N_HEADS, HEAD_DIM).transpose(0, 2, 1, 3)
        q, k, v = (to_heads(q), to_heads(k), to_heads(v))
        q = apply_rotary(q)
        k = apply_rotary(k)
        scores = jnp.einsum('bhqd,bhkd->bhqk', q, k) * SCALE
        weights = jax.nn.softmax(scores, axis=-1)
        attn = jnp.einsum('bhqk,bhkd->bhqd', weights, v)
        attn = attn.transpose(0, 2, 1, 3).reshape(B, T, D)
        return attn @ out_w + out_b

    def _L0_ffn_ref(x, ln_gamma, ln_beta, fc1_q, fc1_scales, fc1_bias, fc2_q, fc2_scales, fc2_bias):
        import jax, jax.numpy as jnp
        import numpy as np
        B, S, H, F, G = (8, 256, 128, 512, 128)
        EPS = 1e-05

        def _dequant(q, scales, g):
            K, N = q.shape
            w = (q.astype(jnp.float32) - 128.0).reshape(K // g, g, N) * scales[:, None, :]
            return w.reshape(K, N)
        residual = x
        mu = jnp.mean(x, axis=-1, keepdims=True)
        var = jnp.mean(jnp.square(x - mu), axis=-1, keepdims=True)
        h = (x - mu) * jax.lax.rsqrt(var + EPS) * ln_gamma + ln_beta
        hf = h.reshape(-1, H)
        w1 = _dequant(fc1_q, fc1_scales, G)
        y = hf @ w1 + fc1_bias
        y = jax.nn.silu(y)
        w2 = _dequant(fc2_q, fc2_scales, G)
        z = y @ w2 + fc2_bias
        return residual + 0.5 * z.reshape(residual.shape)
    x = L0_attn_a_x
    x = x + _L0_attn_a_ref(_layernorm(x, axis=-1), L0_attn_a_qkv_w, L0_attn_a_qkv_b, L0_attn_a_out_w, L0_attn_a_out_b)
    x = x + _L0_ffn_ref(_layernorm(x, axis=-1), L0_ffn_ln_gamma, L0_ffn_ln_beta, L0_ffn_fc1_q, L0_ffn_fc1_scales, L0_ffn_fc1_bias, L0_ffn_fc2_q, L0_ffn_fc2_scales, L0_ffn_fc2_bias)
    x = x + _L0_attn_b_ref(_layernorm(x, axis=-1), L0_attn_b_qkv_w, L0_attn_b_qkv_b, L0_attn_b_out_w, L0_attn_b_out_b)
    x = x + _L0_ffn_ref(_layernorm(x, axis=-1), L0_ffn_ln_gamma, L0_ffn_ln_beta, L0_ffn_fc1_q, L0_ffn_fc1_scales, L0_ffn_fc1_bias, L0_ffn_fc2_q, L0_ffn_fc2_scales, L0_ffn_fc2_bias)
    return x

_drawn_inputs = setup_inputs


def setup_inputs(seed=0):
    import zlib

    import numpy as np

    out = dict(_drawn_inputs(seed))
    spreads = {'L0_attn_a_qkv_b': (0.0, 0.1),
     'L0_attn_a_out_b': (0.0, 0.1),
     'L0_attn_b_qkv_b': (0.0, 0.8),
     'L0_attn_b_out_b': (0.0, 0.8),
     'L0_ffn_ln_gamma': (1.0, 0.2),
     'L0_ffn_ln_beta': (0.0, 0.1)}
    factors = {'L0_attn_b_qkv_w': 8.0,
     'L0_attn_b_out_w': 8.0,
     'L0_ffn_fc1_bias': 8.0,
     'L0_ffn_fc2_bias': 8.0}
    for name, (base, spread) in spreads.items():
        noise = np.random.default_rng([zlib.crc32(name.encode()), seed]).standard_normal(out[name].shape)
        drawn = base * np.exp(spread * noise) if base else spread * noise
        out[name] = jnp.asarray(drawn.astype(out[name].dtype))
    for name, factor in factors.items():
        out[name] = (out[name] * factor).astype(out[name].dtype)
    return out
```

```python
from contextlib import ExitStack

import concourse.bass as bass
from concourse import mybir
from concourse.alu_op_type import AluOpType as ALU

F32 = mybir.dt.float32
BF16 = mybir.dt.bfloat16
I32 = mybir.dt.int32
ACT = mybir.ActivationFunctionType
AX_X = mybir.AxisListType.X

P = 128
BATCH, TOK, D = 16, 512, 128
HEADS, HD = 16, 8
FF = 512
LAYERS = 2
ITEMS = LAYERS * BATCH
R = TOK // P
QUADS = 4
FC = FF // P
UNITS = HEADS * R
SLOTS = QUADS * R
QK_ROWS = 8
MAX_ROW = 7
VCOLS = 32
SCALE = HD ** -0.5
EPS = 1e-5
RING = 3
PBUF = 4


def wait_past(eng, sem, value):
    if not isinstance(value, int) or value > 0:
        eng.wait_ge(sem, value)


def pass_alone(eng, passed):
    eng.sem_inc(passed, 1)


def ring_before(i):
    return i - RING if i >= RING else [63, 61, 62][i] - UNITS


def stages(T):
    return dict(ln=0 <= T + 3 < ITEMS, proj=0 <= T + 2 < ITEMS, mx=0 <= T + 1 < ITEMS,
                attn=0 <= T < ITEMS, out=0 <= T - 1 < ITEMS, ffn=0 <= T - 2 < ITEMS)


STEADY = dict(ln=True, proj=True, mx=True, attn=True, out=True, ffn=True)
FC1_SLOTS, V_SLOT, XT_SLOT, ROT_SLOTS, OUT_SLOT, FC2_SLOT, HT_SLOT = [0, 2, 8, 10], 1, 3, [4, 5, 6, 7], 9, 12, 14
MAXT_SLOTS = [6, 10, 14, 2]
O_SLOTS = [5, 9, 13, 1]
PART_SLOTS = [(0, 0, 7), (0, 1, 8), (1, 0, 9), (1, 1, 11)]
LOOP_FROM, LOOP_TO = 4, 28
FIRST, LAST = -3, ITEMS + 1


def run_bodies(eng, body):
    for T in range(FIRST, LOOP_FROM):
        body(T, T % 2, stages(T))
    with eng.Fori(LOOP_FROM // 2, LOOP_TO // 2) as u:
        body(2 * u, 0, STEADY)
        body(2 * u + 1, 1, STEADY)
    for T in range(LOOP_TO, LAST + 1):
        body(T, T % 2, stages(T))


def hybrid_layers(nc, x, w_attn, b_rot, b_v, b_out, gamma, beta, fc1_q, fc1_s, fc1_b, fc2_q, fc2_s, fc2_b,
                  cos_t, sin_t, ident_t, out):
    with ExitStack() as ctx:
        def sb(name, shape, dt=F32):
            return ctx.enter_context(nc.sbuf_tensor(name, shape, dt))

        def ps(name, shape, dt=F32):
            return ctx.enter_context(nc.psum_tensor(name, shape, dt))

        def sem(name):
            return ctx.enter_context(nc.semaphore(name))

        hidden = nc.dram_tensor("hidden", (BATCH, P, R * D), F32, kind="Internal").ap()
        qk_dram = nc.dram_tensor("qk_dram", (2, P, QK_ROWS, TOK), BF16, kind="Internal").ap()
        o_dram = nc.dram_tensor("o_dram", (QUADS, 4, VCOLS, TOK), F32, kind="Internal").ap()
        l_dram = nc.dram_tensor("l_dram", (P, TOK // HD), F32, kind="Internal").ap()

        ident = sb("ident", [P, P])
        ident_bf = sb("ident_bf", [P, P], BF16)
        cos_sb = sb("cos_sb", [P, TOK])
        sin_sb = sb("sin_sb", [P, TOK])
        w_proj = sb("w_proj", [P, 5, D])
        w_out = sb("w_out", [P, D])
        rot_bias = sb("rot_bias", [P, 4])
        v_bias = sb("v_bias", [P, R, D])
        out_bias = sb("out_bias", [P, R, D])
        gamma_sb = sb("gamma_sb", [P, 1])
        beta_sb = sb("beta_sb", [P, 1])
        q1_int = sb("q1_int", [P, FF], I32)
        q2_int = sb("q2_int", [P, FC, D], I32)
        s1 = sb("s1", [P, FF])
        s2 = sb("s2", [P, FC, D])
        w1 = sb("w1", [P, FF])
        w2 = sb("w2", [P, FC, D])
        fc1_bias = sb("fc1_bias", [P, FC])
        fc1_bias_half = sb("fc1_bias_half", [P, FC])
        fc2_bias_in = sb("fc2_bias_in", [P, R, D])
        fc2_bias_half = sb("fc2_bias_half", [P, R, D])
        neg_half = sb("neg_half", [P, R])
        fill = sb("fill", [P, 2, TOK], BF16)

        x_in = sb("x_in", [P, R, D])
        xn = sb("xn", [P, R, D])
        xnT = sb("xnT", [P, TOK])
        rope_a = sb("rope_a", [P, TOK])
        rope_b = sb("rope_b", [P, TOK])
        rotated = [sb("q_rot", [P, TOK]), sb("k_rot", [P, TOK])]
        rest = [sb("q_rest", [P, TOK]), sb("k_rest", [P, TOK])]
        parts = [sb("q_parts", [P, 3, TOK], BF16), sb("k_parts", [P, 3, TOK], BF16)]
        q_stack = [sb(f"q_stack{i}", [P, HEADS // 2, TOK], BF16) for i in range(2)]
        k_stack = [sb(f"k_stack{i}", [P, HEADS // 2, TOK], BF16) for i in range(2)]
        v_sb = [sb(f"v_sb{i}", [P, R, HEADS, VCOLS]) for i in range(2)]
        neg_max = sb("neg_max", [P, QUADS, R, 2, 2])
        max_parts = sb("max_parts", [P, R, 2, 3, 2], BF16)
        max_rest = sb("max_rest", [P, R, 2, 2])
        max_rows = sb("max_rows", [12, 2, TOK], BF16)
        probs = sb("probs", [P, PBUF, 4, TOK])
        o_sb = sb("o_sb", [P, 2, TOK])
        l_sb = sb("l_sb", [P, TOK // HD])
        l_inv = sb("l_inv", [P, TOK // HD])
        l_bc = sb("l_bc", [P, TOK])
        attn_raw = sb("attn_raw", [P, TOK])
        attnT = sb("attnT", [P, TOK])
        x_res = sb("x_res", [P, R, D])
        x_biased = sb("x_biased", [P, R, D])
        x1 = sb("x1", [P, R, D])
        h0 = sb("h0", [P, R, D])
        hn = sb("hn", [P, R, D])
        hT = sb("hT", [P, TOK])
        fc1_y = sb("fc1_y", [P, 2, TOK])
        fc1_t = sb("fc1_t", [P, 2, TOK])
        act_sb = sb("act_sb", [P, FC, TOK])
        x1_h0 = sb("x1_h0", [P, R, D])
        x2_base = sb("x2_base", [P, R, D])
        x2 = sb("x2", [P, R, D])
        LN_IN, LN_A, LN_B = range(3)
        stats = sb("stats", [P, 3, R, 6])
        mean_var = sb("mean_var", [P, 3, R, 2])
        var_eps = sb("var_eps", [P, 3, R])
        rstd = sb("rstd", [P, 3, R])

        s_bank = [ps(f"s_bank{i}", [P, TOK]) for i in range(RING)]
        t_bank = [ps(f"t_bank{i}", [P, TOK]) for i in range(RING)]
        o_bank = ps("o_bank", [P, TOK])
        misc = ps("misc", [P, TOK])
        misc_bf = misc[:, 0:TOK // 2].bitcast(BF16)

        const_loaded = sem("const_loaded")
        fill_ready = sem("fill_ready")
        fill_written = sem("fill_written")
        dve_setup = sem("dve_setup")
        pool_setup = sem("pool_setup")
        proj_w_loaded = sem("proj_w_loaded")
        out_w_loaded = sem("out_w_loaded")
        proj_w_ok = sem("proj_w_ok")
        out_w_ok = sem("out_w_ok")
        x_in_loaded = sem("x_in_loaded")
        ln_stat = [sem(f"ln_stat{i}") for i in range(3)]
        ln_rstd = [sem(f"ln_rstd{i}") for i in range(3)]
        ln_norm = [sem(f"ln_norm{i}") for i in range(3)]
        xT_ready = sem("xT_ready")
        xT_copied = sem("xT_copied")
        rot_ready = sem("rot_ready")
        rope_done = sem("rope_done")
        rope_sum = sem("rope_sum")
        part_copied = sem("part_copied")
        part_rest = sem("part_rest")
        parts_written = sem("parts_written")
        stack_loaded = [sem(f"stack_loaded{g}") for g in range(QUADS)]
        v_ready = sem("v_ready")
        v_done = sem("v_done")
        s_ready = sem("s_ready")
        s_max = sem("s_max")
        max_split = sem("max_split")
        maxT_ready = sem("maxT_ready")
        maxT_copied = sem("maxT_copied")
        max_rows_loaded = [sem(f"max_rows_loaded{g}") for g in range(QUADS)]
        t_ready = sem("t_ready")
        exp_done = sem("exp_done")
        pv_done = sem("pv_done")
        o_copied = sem("o_copied")
        o_written = [sem(f"o_written{i}") for i in range(2)]
        l_loaded = sem("l_loaded")
        o_loaded = sem("o_loaded")
        l_inverted = sem("l_inverted")
        l_written = sem("l_written")
        l_bc_loaded = sem("l_bc_loaded")
        attn_scaled = sem("attn_scaled")
        x_res_loaded = sem("x_res_loaded")
        x_biased_done = sem("x_biased_done")
        out_ready = sem("out_ready")
        x1_done = sem("x1_done")
        hT_ready = sem("hT_ready")
        hT_copied = sem("hT_copied")
        fc1_ready = sem("fc1_ready")
        fc1_copied = sem("fc1_copied")
        silu_done = sem("silu_done")
        x2_base_done = sem("x2_base_done")
        fc2_ready = sem("fc2_ready")
        x2_done = sem("x2_done")
        stored = sem("stored")

        sp_passed = sem("sp_passed")
        dve_passed = sem("dve_passed")
        pool_passed = sem("pool_passed")

        block = ctx.enter_context(nc.Block())
        n_const = 14

        @block.sync
        def _(sp):
            for dst, src in (
                (ident[:, :], ident_t), (cos_sb[:, :], cos_t), (sin_sb[:, :], sin_t),
                (gamma_sb[:, :], gamma), (beta_sb[:, :], beta),
                (q1_int[:, :], fc1_q), (s1[:, :], fc1_s.to_broadcast([P, FF])),
                (q2_int[:, :, :], fc2_q.rearrange("(c p) n -> p c n", p=P)),
                (fc1_bias[:, :], fc1_b),
            ):
                sp.dma_start(dst, src).then_inc(const_loaded, 16)
            sp.dma_start(s2[:, :, :].rearrange("p c n -> p (c n)"), fc2_s.to_broadcast([P, FF])).then_inc(const_loaded, 16)
            for r in range(R):
                sp.dma_start(fc2_bias_in[:, r, :], fc2_b.to_broadcast([P, D])).then_inc(const_loaded, 16)
            sp.wait_ge(fill_ready, 2)
            for s in range(2):
                sp.dma_start(qk_dram[s, :, MAX_ROW, :], fill[:, s, :]).then_inc(fill_written, 16)
            sp.wait_ge(fill_written, 32)

            def load_proj_weights(layer):
                sp.dma_start(w_proj[:, :, :], w_attn[layer, :, 0:5, :]).then_inc(proj_w_loaded, 16)
                sp.dma_start(rot_bias[:, :], b_rot[layer]).then_inc(proj_w_loaded, 16)
                for r in range(R):
                    sp.dma_start(v_bias[:, r, :], b_v[layer:layer + 1].to_broadcast([P, D])).then_inc(proj_w_loaded, 16)
                sp.wait_ge(proj_w_loaded, 96 * (layer + 1))

            def load_out_weights(layer):
                sp.dma_start(w_out[:, :], w_attn[layer, :, 5, :]).then_inc(out_w_loaded, 16)
                for r in range(R):
                    sp.dma_start(out_bias[:, r, :], b_out[layer:layer + 1].to_broadcast([P, D])).then_inc(out_w_loaded, 16)
                sp.wait_ge(out_w_loaded, 80 * (layer + 1))

            def rows_of(b, layer):
                return x[b] if layer == 0 else hidden[b - BATCH]

            def max_rows_in(b, par, g):
                sp.wait_ge(maxT_copied, 4 * b + g + 1)
                for s in range(2):
                    sp.dma_start(q_stack[par][64 * s + MAX_ROW:64 * s + MAX_ROW + 3 * HD:HD, 2 * g:2 * g + 2, :],
                                 max_rows[6 * s:6 * s + 6, g % 2, :]).then_inc(max_rows_loaded[g], 16)

            def o_out(b, g):
                if g == 0:
                    wait_past(sp, l_loaded, 16 * b)
                    wait_past(sp, o_loaded, 16 * b)
                sp.wait_ge(o_copied, 4 * b + g + 1)
                sp.dma_start(o_dram[g].rearrange("j c n -> (j c) n"), o_sb[:, g % 2, :]).then_inc(o_written[g % 2], 16)

            def stack_in(b, par, g):
                wait_past(sp, t_ready, UNITS * (b - 2) + 16 * (g + 1))
                for side, dst in ((0, q_stack[par]), (1, k_stack[par])):
                    src = qk_dram[side].rearrange("(p s d) t n -> p (s d t) n", s=2, d=HD)
                    sp.dma_start(dst[:, 2 * g:2 * g + 2, :],
                                 src[2 * g:2 * g + 2].rearrange("p r n -> r p n")).then_inc(stack_loaded[g], 16)

            def body(T, par, on, in_layer=0, res_layer=0, store_layer=0, reload_proj=False, reload_out=False):
                if on["ln"]:
                    b = T + 3
                    wait_past(sp, ln_norm[LN_IN], b)
                    if in_layer:
                        sp.wait_ge(stored, 16 * (b - BATCH + 1))
                    pass_alone(sp, sp_passed)
                    sp.dma_start(x_in[:, :, :].rearrange("p r d -> p (r d)"), rows_of(b, in_layer)).then_inc(x_in_loaded, 16)
                if on["proj"]:
                    if reload_proj:
                        sp.wait_ge(v_done, BATCH)
                        load_proj_weights(1)
                    sp.sem_inc(proj_w_ok, 1)
                if on["out"]:
                    b = T - 1
                    o_out(b, 3)
                    for i in range(2):
                        sp.wait_ge(o_written[i], 32 * (b + 1))
                    pass_alone(sp, sp_passed)
                    wait_past(sp, l_inverted, b)
                    sp.dma_start(l_sb[:, :], o_dram[:, :, HD, :].rearrange("g j (a n) -> (g j) a n", a=HD)).then_inc(l_loaded, 16)
                    wait_past(sp, attn_scaled, b)
                    sp.dma_start(attn_raw[:, :], o_dram[:, :, 0:HD, :].rearrange("g j d n -> (g j) d n")).then_inc(o_loaded, 16)
                if on["attn"]:
                    max_rows_in(T, par, 3)
                if on["out"]:
                    b = T - 1
                    sp.wait_ge(l_inverted, b + 1)
                    wait_past(sp, l_bc_loaded, 16 * b)
                    sp.dma_start(l_dram, l_inv[:, :]).then_inc(l_written, 16)
                    sp.wait_ge(l_written, 16 * (b + 1))
                    sp.dma_start(l_bc[:, :], l_dram.rearrange("(h a) (o n) -> h o (a n)", a=HD, o=1)
                                 .to_broadcast([HEADS, HD, TOK])).then_inc(l_bc_loaded, 16)
                if on["attn"]:
                    wait_past(sp, x_biased_done, T)
                    if res_layer:
                        sp.wait_ge(stored, 16 * (T - BATCH + 1))
                    pass_alone(sp, sp_passed)
                    sp.dma_start(x_res[:, :, :].rearrange("p r d -> p (r d)"), rows_of(T, res_layer)).then_inc(x_res_loaded, 16)
                    o_out(T, 0)
                if on["mx"]:
                    max_rows_in(T + 1, 1 - par, 0)
                if on["proj"]:
                    b = T + 2
                    for g in range(QUADS):
                        wait_past(sp, stack_loaded[g], 32 * b)
                    sp.wait_ge(part_rest, 4 * b + 2)
                    qp, kp = parts
                    for n, t, m in ((0, 0, 3), (1, 3, 3), (2, 6, 1)):
                        sp.dma_start(qk_dram[0, :, t:t + m, :], qp[:, n:n + 1, :].to_broadcast([P, m, TOK])).then_inc(parts_written, 16)
                if on["attn"]:
                    o_out(T, 1)
                if on["mx"]:
                    max_rows_in(T + 1, 1 - par, 1)
                if on["proj"]:
                    b = T + 2
                    sp.wait_ge(part_rest, 4 * b + 4)
                    sp.dma_start(qk_dram[1, :, 0:3, :], kp[:, :, :]).then_inc(parts_written, 16)
                    sp.dma_start(qk_dram[1, :, 3:6, :], kp[:, :, :]).then_inc(parts_written, 16)
                    sp.dma_start(qk_dram[1, :, 6, :], kp[:, 0, :]).then_inc(parts_written, 16)
                    sp.wait_ge(parts_written, 96 * (b + 1))
                    stack_in(b, par, 0)
                    stack_in(b, par, 1)
                if on["attn"]:
                    o_out(T, 2)
                if on["ffn"]:
                    b = T - 2
                    sp.wait_ge(x2_done, b + 1)
                    pass_alone(sp, sp_passed)
                    dst = hidden[b] if store_layer == 0 else out[b - BATCH]
                    sp.dma_start(dst, x2[:, :, :].rearrange("p r d -> p (r d)")).then_inc(stored, 16)
                if on["mx"]:
                    max_rows_in(T + 1, 1 - par, 2)
                if on["attn"]:
                    if reload_out:
                        sp.wait_ge(out_ready, BATCH)
                        sp.wait_ge(x_biased_done, BATCH)
                        load_out_weights(1)
                    sp.sem_inc(out_w_ok, 1)
                if on["proj"]:
                    stack_in(T + 2, par, 2)
                    stack_in(T + 2, par, 3)

            load_proj_weights(0)
            load_out_weights(0)

            def single(T):
                body(T, T % 2, stages(T), in_layer=int(T + 3 >= BATCH), res_layer=int(T >= BATCH),
                     store_layer=int(T - 2 >= BATCH), reload_proj=T + 2 == BATCH, reload_out=T == BATCH)

            for T in range(FIRST, LOOP_FROM):
                single(T)
            with sp.Fori(LOOP_FROM // 2, 6) as u:
                body(2 * u, 0, STEADY)
                body(2 * u + 1, 1, STEADY)
            for T in range(12, BATCH + 2):
                single(T)
            with sp.Fori(BATCH // 2 + 1, LOOP_TO // 2) as u:
                body(2 * u, 0, STEADY, 1, 1, 1)
                body(2 * u + 1, 1, STEADY, 1, 1, 1)
            for T in range(LOOP_TO, LAST + 1):
                single(T)
            sp.wait_ge(stored, 16 * ITEMS)

        @block.tensor
        def _(pe):
            last_misc = [None]

            def misc_free():
                if last_misc[0] is not None:
                    wait_past(pe, *last_misc[0])

            def body(T, par, on):
                def score_max_pair(g, qt, a):
                    b = T + 1
                    if qt == 0 and a == 0:
                        pe.wait_ge(stack_loaded[g], 32 * (b + 1))
                    for s in range(2):
                        i = 16 * g + 4 * qt + 2 * a + s
                        wait_past(pe, s_max, UNITS * b + ring_before(i) + 1)
                        rows = slice(64 * s, 64 * s + 64)
                        nc.tensor.matmul(s_bank[i % RING][:, :], q_stack[1 - par][rows, 2 * g + a, qt * P:(qt + 1) * P],
                                         k_stack[1 - par][rows, 2 * g + a, :], start=True, stop=True).then_inc(s_ready, 1)

                def score_exp_pair(g, kc, a):
                    b = T
                    if kc == 0 and a == 0:
                        pe.wait_ge(max_rows_loaded[g], 32 * (b + 1))
                    for s in range(2):
                        i = 16 * g + 4 * kc + 2 * a + s
                        wait_past(pe, exp_done, UNITS * b + ring_before(i) + 1)
                        rows = slice(64 * s, 64 * s + 64)
                        nc.tensor.matmul(t_bank[i % RING][:, :], k_stack[par][rows, 2 * g + a, kc * P:(kc + 1) * P],
                                         q_stack[par][rows, 2 * g + a, :], start=True, stop=True).then_inc(t_ready, 1)

                def weighted_sum(b, vpar, k):
                    g, kc = divmod(k, R)
                    if k == 0:
                        pe.wait_ge(v_done, b + 1)
                    if kc == 0:
                        wait_past(pe, o_copied, 4 * b + g)
                    pe.wait_ge(exp_done, UNITS * b + 4 * (k + 1))
                    for j in range(4):
                        mm = nc.tensor.matmul(o_bank[32 * j:32 * j + 32, :], v_sb[vpar][:, kc, 4 * g + j, :],
                                              probs[:, k % PBUF, j, :], start=kc == 0, stop=kc == R - 1)
                    mm.then_inc(pv_done, 1)

                def transpose_rows(src, b, normed, ready, copied):
                    pe.wait_ge(normed, b + 1)
                    misc_free()
                    for r in range(R):
                        mm = nc.tensor.transpose(misc[:, r * P:(r + 1) * P], src[:, r, :], ident[:, :])
                    mm.then_inc(ready, 1)
                    last_misc[0] = (copied, b + 1)

                def project_rot(n):
                    b = T + 2
                    if n == 0:
                        pe.wait_ge(proj_w_ok, b + 1)
                        pe.wait_ge(xT_copied, b + 1)
                    misc_free()
                    nc.tensor.matmul(misc[:, :], w_proj[:, n, :], xnT[:, :], start=True, stop=True).then_inc(rot_ready, 1)
                    last_misc[0] = (rope_done, 4 * b + n + 1)

                def project_v():
                    b = T + 1
                    misc_free()
                    for r in range(R):
                        mm = nc.tensor.matmul(misc[:, r * P:(r + 1) * P], xnT[:, r * P:(r + 1) * P], w_proj[:, 4, :],
                                              start=True, stop=True)
                    mm.then_inc(v_ready, 1)
                    last_misc[0] = (v_done, b + 1)

                def max_to_rows(b, g):
                    pe.wait_ge(max_split, 16 * b + 4 * g + 4)
                    misc_free()
                    for r in range(R):
                        mm = nc.tensor.transpose(misc_bf[0:12, r * P:(r + 1) * P],
                                                 max_parts[:, r, :, :, :].rearrange("p s n a -> p (s n a)"), ident_bf[:, :])
                    mm.then_inc(maxT_ready, 1)
                    last_misc[0] = (maxT_copied, 4 * b + g + 1)

                def project_out():
                    b = T - 1
                    pe.wait_ge(attn_scaled, b + 1)
                    pe.wait_ge(out_w_ok, b + 1)
                    misc_free()
                    for r in range(R):
                        mm = nc.tensor.matmul(misc[:, r * P:(r + 1) * P], attnT[:, r * P:(r + 1) * P], w_out[:, :],
                                              start=True, stop=True)
                    mm.then_inc(out_ready, 1)
                    last_misc[0] = (x1_done, b + 1)

                def fc1(c):
                    b = T - 2
                    if c == 0:
                        pe.wait_ge(hT_copied, b + 1)
                    misc_free()
                    nc.tensor.matmul(misc[:, :], w1[:, c * P:(c + 1) * P], hT[:, :], start=True, stop=True).then_inc(fc1_ready, 1)
                    last_misc[0] = (fc1_copied, 4 * b + c + 1)

                def fc2(half):
                    b = T - 2
                    if half == 0:
                        pe.wait_ge(silu_done, 4 * (b + 1))
                        misc_free()
                    for r in range(2 * half, 2 * half + 2):
                        for c in range(FC):
                            mm = nc.tensor.matmul(misc[:, r * P:(r + 1) * P], act_sb[:, c, r * P:(r + 1) * P], w2[:, c, :],
                                                  start=c == 0, stop=c == FC - 1)
                    if half == 1:
                        mm.then_inc(fc2_ready, 1)
                        last_misc[0] = (x2_done, b + 1)

                for k in range(SLOTS):
                    g, n = divmod(k, R)
                    if on["attn"]:
                        score_exp_pair(g, n, 0)
                    if on["mx"]:
                        score_max_pair(g, n, 0)
                    if k in FC1_SLOTS and on["ffn"]:
                        fc1(FC1_SLOTS.index(k))
                    if k == V_SLOT and on["mx"]:
                        project_v()
                    if k == XT_SLOT and on["proj"]:
                        transpose_rows(xn, T + 2, ln_norm[LN_IN], xT_ready, xT_copied)
                    if k in ROT_SLOTS and on["proj"]:
                        project_rot(k - ROT_SLOTS[0])
                    if k == OUT_SLOT and on["out"]:
                        project_out()
                    if k == FC2_SLOT and on["ffn"]:
                        fc2(0)
                    if k == HT_SLOT and on["out"]:
                        transpose_rows(hn, T - 1, ln_norm[LN_B], hT_ready, hT_copied)
                    if on["attn"]:
                        score_exp_pair(g, n, 1)
                    if on["mx"]:
                        score_max_pair(g, n, 1)
                    if k == FC2_SLOT and on["ffn"]:
                        fc2(1)
                    if k == MAXT_SLOTS[3] and on["attn"]:
                        max_to_rows(T, 3)
                    if k in MAXT_SLOTS[0:3] and on["mx"]:
                        max_to_rows(T + 1, MAXT_SLOTS.index(k))
                    if k == 0 and on["out"]:
                        weighted_sum(T - 1, 1 - par, SLOTS - 1)
                    if k > 0 and on["attn"]:
                        weighted_sum(T, par, k - 1)

            pe.wait_ge(dve_setup, 8)
            run_bodies(pe, body)

        @block.scalar
        def _(act):
            act.wait_ge(dve_setup, 8)

            def body(T, par, on):
                def exps(k, a):
                    if a == 0:
                        wait_past(act, pv_done, 16 * T + k + 1 - PBUF)
                    for s in range(2):
                        i = 4 * k + 2 * a + s
                        act.wait_ge(t_ready, UNITS * T + i + 1)
                        nc.scalar.activation(probs[:, k % PBUF, 2 * a + s, :], t_bank[i % RING][:, :], ACT.Exp,
                                             scale=SCALE).then_inc(exp_done, 1)

                def max_rows_copy(b, g):
                    act.wait_ge(maxT_ready, 4 * b + g + 1)
                    wait_past(act, max_rows_loaded[(g + 2) % 4], 32 * (b + g // 2))
                    nc.scalar.copy(max_rows[:, g % 2, :], misc_bf[0:12, :]).then_inc(maxT_copied, 1)

                def o_copy(b, g):
                    act.wait_ge(pv_done, 16 * b + 4 * (g + 1))
                    wait_past(act, o_written[g % 2], 32 * b + 16 * (g // 2))
                    nc.scalar.copy(o_sb[:, g % 2, :], o_bank[:, :]).then_inc(o_copied, 1)

                def part_copy(side, n):
                    b = T + 2
                    if side == 0 and n == 0:
                        wait_past(act, parts_written, 96 * b)
                    if n == 0:
                        act.wait_ge(rope_sum, 2 * b + side + 1)
                    else:
                        act.wait_ge(part_rest, 4 * b + 2 * side + 1)
                    src = rotated[side] if n == 0 else rest[side]
                    nc.scalar.copy(parts[side][:, n, :], src[:, :]).then_inc(part_copied, 1)

                def silu_terms(c):
                    b = T - 2
                    act.wait_ge(fc1_ready, 4 * b + c + 1)
                    wait_past(act, silu_done, 4 * b + c - 1)
                    nc.scalar.activation(fc1_y[:, c % 2, :], misc[:, :], ACT.Identity, bias=fc1_bias[:, c:c + 1])
                    nc.scalar.activation(fc1_t[:, c % 2, :], misc[:, :], ACT.Tanh, bias=fc1_bias_half[:, c:c + 1],
                                         scale=0.5).then_inc(fc1_copied, 1)

                for k in range(SLOTS):
                    if on["attn"]:
                        exps(k, 0)
                    if k == O_SLOTS[3] and on["out"]:
                        o_copy(T - 1, 3)
                    if k in O_SLOTS[0:3] and on["attn"]:
                        o_copy(T, O_SLOTS.index(k))
                    if k in FC1_SLOTS and on["ffn"]:
                        silu_terms(FC1_SLOTS.index(k))
                    if k == XT_SLOT and on["proj"]:
                        act.wait_ge(xT_ready, T + 3)
                        wait_past(act, v_ready, T + 2)
                        nc.scalar.copy(xnT[:, :], misc[:, :]).then_inc(xT_copied, 1)
                    if k == HT_SLOT and on["out"]:
                        b = T - 1
                        act.wait_ge(hT_ready, b + 1)
                        wait_past(act, fc1_ready, 4 * b)
                        nc.scalar.activation(hT[:, :], misc[:, :], ACT.Identity, bias=beta_sb[:, 0:1],
                                             scale=gamma_sb[:, 0:1]).then_inc(hT_copied, 1)
                    for side, n, slot in PART_SLOTS:
                        if k == slot and on["proj"]:
                            part_copy(side, n)
                    if on["attn"]:
                        exps(k, 1)
                    if k == MAXT_SLOTS[3] and on["attn"]:
                        max_rows_copy(T, 3)
                    if k in MAXT_SLOTS[0:3] and on["mx"]:
                        max_rows_copy(T + 1, MAXT_SLOTS.index(k))

            run_bodies(act, body)

        @block.vector
        def _(dve):
            nc.vector.memset(fill[:, 0, :], 0.0).then_inc(fill_ready, 1)
            nc.vector.memset(fill[:, 1, :], 1.0).then_inc(fill_ready, 1)
            for i in range(2):
                nc.vector.memset(v_sb[i][:, :, :, :], 0.0).then_inc(dve_setup, 1)
            dve.wait_ge(dve_setup, 2)
            for i in range(2):
                nc.vector.memset(v_sb[i][:, :, :, HD:HD + 1], 1.0).then_inc(dve_setup, 1)
            dve.wait_ge(const_loaded, 16 * n_const)
            nc.vector.tensor_copy(ident_bf[:, :], ident[:, :])
            nc.vector.scalar_tensor_tensor(out=w1[:, :], in0=q1_int[:, :], scalar=-128.0, in1=s1[:, :],
                                           op0=ALU.add, op1=ALU.mult).then_inc(dve_setup, 1)
            nc.vector.scalar_tensor_tensor(out=w2[:, :, :], in0=q2_int[:, :, :], scalar=-128.0, in1=s2[:, :, :],
                                           op0=ALU.add, op1=ALU.mult).then_inc(dve_setup, 1)
            dve.wait_ge(dve_setup, 6)
            nc.vector.tensor_scalar(w2[:, :, :], w2[:, :, :], 0.25, None, ALU.mult).then_inc(dve_setup, 1)
            nc.vector.tensor_scalar(fc1_bias_half[:, :], fc1_bias[:, :], 0.5, None, ALU.mult)
            nc.vector.tensor_scalar(fc2_bias_half[:, :, :], fc2_bias_in[:, :, :], 0.5, None, ALU.mult).then_inc(dve_setup, 1)

            def layer_norm_stats(which, src, b):
                for r in range(R):
                    st = nc.vector.bn_stats(stats[:, which, r, :], src[:, r, :])
                st.then_inc(ln_stat[which], 1)
                dve.wait_ge(ln_stat[which], 3 * b + 1)
                pass_alone(dve, dve_passed)
                for r in range(R):
                    ag = nc.vector.bn_aggr(mean_var[:, which, r, :], stats[:, which, r, :])
                ag.then_inc(ln_stat[which], 1)
                dve.wait_ge(ln_stat[which], 3 * b + 2)
                nc.vector.tensor_scalar(var_eps[:, which, :], mean_var[:, which, :, 1], EPS, None, ALU.add)\
                    .then_inc(ln_stat[which], 1)

            def layer_norm_apply(which, dst, src, b):
                dve.wait_ge(ln_rstd[which], b + 1)
                for r in range(R):
                    nm = nc.vector.tensor_scalar(dst[:, r, :], src[:, r, :], mean_var[:, which, r, 0:1],
                                                 rstd[:, which, r:r + 1], ALU.subtract, ALU.mult)
                nm.then_inc(ln_norm[which], 1)

            def body(T, par, on):
                def maxima(k, a):
                    b = T + 1
                    g, qt = divmod(k, R)
                    if qt == 0 and a == 0:
                        wait_past(dve, max_split, 16 * (b - 1) + 4 * g + 2)
                    for s in range(2):
                        i = 4 * k + 2 * a + s
                        dve.wait_ge(s_ready, UNITS * b + i + 1)
                        nc.vector.tensor_reduce(neg_max[:, g, qt, s, a:a + 1], s_bank[i % RING][:, :], AX_X, ALU.max,
                                                negate=True).then_inc(s_max, 1)

                def rope(n):
                    b = T + 2
                    dve.wait_ge(rot_ready, 4 * b + n + 1)
                    if n % 2 == 0:
                        wait_past(dve, rope_sum, 2 * b + n // 2)
                    dst, table = ((rope_a, cos_sb), (rope_b, sin_sb))[n % 2]
                    nc.vector.scalar_tensor_tensor(out=dst[:, :], in0=misc[:, :], scalar=rot_bias[:, n:n + 1],
                                                   in1=table[:, :], op0=ALU.add, op1=ALU.mult).then_inc(rope_done, 1)

                def silu(c):
                    b = T - 2
                    dve.wait_ge(fc1_copied, 4 * b + c + 1)
                    if c == 0:
                        wait_past(dve, fc2_ready, b)
                    nc.vector.scalar_tensor_tensor(out=act_sb[:, c, :], in0=fc1_t[:, c % 2, :], scalar=1.0,
                                                   in1=fc1_y[:, c % 2, :], op0=ALU.add, op1=ALU.mult).then_inc(silu_done, 1)

                for k in range(SLOTS):
                    if on["mx"]:
                        maxima(k, 0)
                    if k == V_SLOT and on["mx"]:
                        b = T + 1
                        dve.wait_ge(v_ready, b + 1)
                        wait_past(dve, pv_done, 16 * (b - 1))
                        nc.vector.tensor_tensor(v_sb[1 - par][:, :, :, 0:HD].rearrange("p r h d -> p (r h) d"),
                                                misc[:, :].rearrange("p (m d) -> p m d", d=HD),
                                                v_bias[:, :, :].rearrange("p r (h d) -> p (r h) d", d=HD),
                                                ALU.add).then_inc(v_done, 1)
                    if k in ROT_SLOTS and on["proj"]:
                        rope(k - ROT_SLOTS[0])
                    if k == OUT_SLOT and on["out"]:
                        b = T - 1
                        dve.wait_ge(out_ready, b + 1)
                        dve.wait_ge(x_biased_done, b + 1)
                        wait_past(dve, x2_base_done, 2 * b)
                        nc.vector.tensor_tensor(x1[:, :, :].rearrange("p r d -> p (r d)"), misc[:, :],
                                                x_biased[:, :, :].rearrange("p r d -> p (r d)"), ALU.add).then_inc(x1_done, 1)
                    if k == FC2_SLOT + 1 and on["ffn"]:
                        b = T - 2
                        dve.wait_ge(fc2_ready, b + 1)
                        dve.wait_ge(x2_base_done, 2 * (b + 1))
                        wait_past(dve, stored, 16 * b)
                        nc.vector.tensor_tensor(x2[:, :, :].rearrange("p r d -> p (r d)"), misc[:, :],
                                                x2_base[:, :, :].rearrange("p r d -> p (r d)"), ALU.add).then_inc(x2_done, 1)
                    if k - 1 in FC1_SLOTS and on["ffn"]:
                        silu(FC1_SLOTS.index(k - 1))
                    if k == 4 and on["out"]:
                        b = T - 1
                        dve.wait_ge(l_loaded, 16 * (b + 1))
                        wait_past(dve, l_written, 16 * b)
                        nc.vector.reciprocal(l_inv[:, :], l_sb[:, :]).then_inc(l_inverted, 1)
                    if k == OUT_SLOT + 1 and on["out"]:
                        dve.wait_ge(x1_done, T)
                        layer_norm_stats(LN_A, x1, T - 1)
                    if k == OUT_SLOT + 2 and on["out"]:
                        layer_norm_apply(LN_A, h0, x1, T - 1)
                        dve.wait_ge(ln_norm[LN_A], T)
                        layer_norm_stats(LN_B, h0, T - 1)
                    if k == OUT_SLOT + 4 and on["out"]:
                        wait_past(dve, hT_ready, T - 1)
                        layer_norm_apply(LN_B, hn, h0, T - 1)
                    if k == 14 and on["ln"]:
                        dve.wait_ge(x_in_loaded, 16 * (T + 4))
                        layer_norm_stats(LN_IN, x_in, T + 3)
                    if on["mx"]:
                        maxima(k, 1)

            run_bodies(dve, body)

        @block.gpsimd
        def _(pool):
            nc.gpsimd.memset(neg_half[:, :], -0.5).then_inc(pool_setup, 1)
            pool.wait_ge(pool_setup, 1)
            pool.wait_ge(dve_setup, 8)

            def inverse_deviation(which, b):
                pool.wait_ge(ln_stat[which], 3 * (b + 1))
                nc.gpsimd.tensor_tensor(rstd[:, which, :], var_eps[:, which, :], neg_half[:, :], ALU.pow)\
                    .then_inc(ln_rstd[which], 1)

            def split_max(b, g):
                n = 16 * b + 4 * g
                pool.wait_ge(s_max, UNITS * b + 16 * (g + 1))
                wait_past(pool, maxT_ready, 4 * b + g)
                pass_alone(pool, pool_passed)
                nc.gpsimd.tensor_copy(max_parts[:, :, :, 0, :], neg_max[:, g, :, :, :]).then_inc(max_split, 1)
                pool.wait_ge(max_split, n + 1)
                nc.gpsimd.tensor_tensor(max_rest[:, :, :, :], neg_max[:, g, :, :, :], max_parts[:, :, :, 0, :],
                                        ALU.subtract).then_inc(max_split, 1)
                pool.wait_ge(max_split, n + 2)
                pass_alone(pool, pool_passed)
                nc.gpsimd.tensor_copy(max_parts[:, :, :, 1, :], max_rest[:, :, :, :]).then_inc(max_split, 1)
                pool.wait_ge(max_split, n + 3)
                nc.gpsimd.tensor_tensor(max_parts[:, :, :, 2, :], max_rest[:, :, :, :], max_parts[:, :, :, 1, :],
                                        ALU.subtract).then_inc(max_split, 1)

            def flat(t):
                return t[:, :, :].rearrange("p r d -> p (r d)")

            def body(T, par, on):
                def rope_add(side):
                    b = T + 2
                    pool.wait_ge(rope_done, 4 * b + 2 * side + 2)
                    wait_past(pool, part_rest, 4 * (b - 1) + 2 * side + 1)
                    nc.gpsimd.tensor_tensor(rotated[side][:, :], rope_a[:, :], rope_b[:, :], ALU.add).then_inc(rope_sum, 1)

                def part_subtract(side, n):
                    b = T + 2
                    pool.wait_ge(part_copied, 4 * b + 2 * side + n + 1)
                    if n == 0:
                        nc.gpsimd.tensor_tensor(rest[side][:, :], rotated[side][:, :], parts[side][:, 0, :],
                                                ALU.subtract).then_inc(part_rest, 1)
                    else:
                        nc.gpsimd.tensor_tensor(parts[side][:, 2, :], rest[side][:, :], parts[side][:, 1, :],
                                                ALU.subtract).then_inc(part_rest, 1)

                if on["attn"]:
                    split_max(T, 3)
                if on["out"]:
                    b = T - 1
                    pool.wait_ge(x_res_loaded, 16 * (b + 1))
                    pool.wait_ge(out_w_ok, b + 1)
                    wait_past(pool, x1_done, b)
                    nc.gpsimd.tensor_tensor(flat(x_biased), flat(x_res), flat(out_bias), ALU.add).then_inc(x_biased_done, 1)
                if on["mx"]:
                    split_max(T + 1, 0)
                if on["proj"]:
                    rope_add(0)
                if on["out"]:
                    b = T - 1
                    pool.wait_ge(o_loaded, 16 * (b + 1))
                    pool.wait_ge(l_bc_loaded, 16 * (b + 1))
                    wait_past(pool, out_ready, b)
                    nc.gpsimd.tensor_tensor(attnT[:, :], attn_raw[:, :], l_bc[:, :], ALU.mult).then_inc(attn_scaled, 1)
                if on["proj"]:
                    part_subtract(0, 0)
                    rope_add(1)
                if on["mx"]:
                    split_max(T + 1, 1)
                if on["proj"]:
                    part_subtract(0, 1)
                    part_subtract(1, 0)
                if on["out"]:
                    inverse_deviation(LN_A, T - 1)
                if on["proj"]:
                    part_subtract(1, 1)
                if on["out"]:
                    inverse_deviation(LN_B, T - 1)
                if on["mx"]:
                    split_max(T + 1, 2)
                if on["out"]:
                    b = T - 1
                    pool.wait_ge(ln_norm[LN_A], b + 1)
                    nc.gpsimd.tensor_tensor(flat(x1_h0), flat(x1), flat(h0), ALU.add).then_inc(x2_base_done, 1)
                    pool.wait_ge(x2_base_done, 2 * b + 1)
                    wait_past(pool, x2_done, b)
                    nc.gpsimd.tensor_tensor(flat(x2_base), flat(x1_h0), flat(fc2_bias_half), ALU.add).then_inc(x2_base_done, 1)
                if on["ln"]:
                    b = T + 3
                    inverse_deviation(LN_IN, b)
                    wait_past(pool, xT_ready, b)
                    pool.wait_ge(ln_rstd[LN_IN], b + 1)
                    pass_alone(pool, pool_passed)
                    for r in range(R):
                        nm = nc.gpsimd.tensor_scalar(xn[:, r, :], x_in[:, r, :], mean_var[:, LN_IN, r, 0:1],
                                                     rstd[:, LN_IN, r:r + 1], ALU.subtract, ALU.mult)
                    nm.then_inc(ln_norm[LN_IN], 1)

            run_bodies(pool, body)


def kernel(**inputs):
    import numpy as np
    from concourse import bacc
    from concourse.bass_utils import run_bass_kernel_spmd

    a = {n: np.asarray(v) for n, v in inputs.items()}

    even, odd = np.arange(0, HD, 2), np.arange(1, HD, 2)
    cols_a = (np.arange(HEADS)[:, None] * HD + np.concatenate([even, odd])[None]).ravel()
    cols_b = (np.arange(HEADS)[:, None] * HD + np.concatenate([odd, even])[None]).ravel()
    w_attn, b_rot, b_v, b_out = [], [], [], []
    for n in ("L0_attn_a", "L0_attn_b"):
        w, wo, b = a[f"{n}_qkv_w"], a[f"{n}_out_w"], a[f"{n}_qkv_b"]
        q, k, v = w[:, 0:D], w[:, D:2 * D], w[:, 2 * D:3 * D]
        w_attn.append(np.stack([q[:, cols_a], q[:, cols_b], k[:, cols_a], k[:, cols_b], v, wo], axis=1))
        bq, bk = b[0:D], b[D:2 * D]
        b_rot.append(np.stack([bq[cols_a], bq[cols_b], bk[cols_a], bk[cols_b]], axis=1))
        b_v.append(b[2 * D:3 * D])
        b_out.append(a[f"{n}_out_b"])

    freqs = (np.float32(10000.0) ** (np.arange(0, HD, 2.0, dtype=np.float32) / HD)).astype(np.float32)
    angles = np.arange(TOK, dtype=np.float32)[:, None] * freqs[None, :]
    order = (np.arange(P)[None, :] * R + np.arange(R)[:, None]).ravel()
    cos, sin = np.cos(angles)[order].T, np.sin(angles)[order].T
    cos_t = np.tile(np.concatenate([cos, cos]), (HEADS, 1)).astype(np.float32)
    sin_t = np.tile(np.concatenate([-sin, sin]), (HEADS, 1)).astype(np.float32)

    arrays = {
        "x": a["L0_attn_a_x"].reshape(BATCH, P, R * D),
        "w_attn": np.stack(w_attn), "b_rot": np.stack(b_rot), "b_v": np.stack(b_v), "b_out": np.stack(b_out),
        "gamma": a["L0_ffn_ln_gamma"].reshape(D, 1), "beta": a["L0_ffn_ln_beta"].reshape(D, 1),
        "fc1_q": a["L0_ffn_fc1_q"], "fc1_s": a["L0_ffn_fc1_scales"].reshape(1, FF),
        "fc1_b": a["L0_ffn_fc1_bias"].reshape(FC, P).T,
        "fc2_q": a["L0_ffn_fc2_q"], "fc2_s": a["L0_ffn_fc2_scales"].reshape(1, FC * D),
        "fc2_b": a["L0_ffn_fc2_bias"].reshape(1, D),
        "cos_t": cos_t, "sin_t": sin_t, "ident_t": np.eye(P, dtype=np.float32),
    }
    arrays = {f"in_{n}": np.ascontiguousarray(v) for n, v in arrays.items()}
    nc = bacc.Bacc("TRN2", target_bir_lowering=False, num_devices=1)
    args = [nc.dram_tensor(n, v.shape, mybir.dt.from_np(v.dtype), kind="ExternalInput").ap() for n, v in arrays.items()]
    args.append(nc.dram_tensor("out_0", (BATCH, P, R * D), F32, kind="ExternalOutput").ap())
    nc.disable_value_cache = True
    hybrid_layers(nc, *args)
    r = run_bass_kernel_spmd(nc, [arrays], core_ids=[0])
    return r.results[0]["out_0"].reshape(BATCH, TOK, D)
```

```python
from contextlib import ExitStack

import concourse.bass as bass
from concourse import mybir
from concourse.alu_op_type import AluOpType as ALU

F32 = mybir.dt.float32
BF16 = mybir.dt.bfloat16
I32 = mybir.dt.int32
ACT = mybir.ActivationFunctionType
AX_X = mybir.AxisListType.X

P = 128
BATCH, TOK, D = 16, 512, 128
HEADS, HD = 16, 8
FF = 512
LAYERS = 2
ITEMS = LAYERS * BATCH
R = TOK // P
QUADS = 4
FC = FF // P
UNITS = HEADS * R
SLOTS = QUADS * R
QK_ROWS = 8
MAX_ROW = 7
VCOLS = 32
SCALE = HD ** -0.5
EPS = 1e-5
RING = 3
HALVES_SWAPPED = [p ^ (HD // 2) for p in range(32)]
PBUF = 4


def per_row(bias):
    return bias.rearrange("u (o n) -> u o n", o=1).to_broadcast([P, R, D])


def wait_past(eng, sem, value):
    if not isinstance(value, int) or value > 0:
        eng.wait_ge(sem, value)


def pass_alone(eng, passed):
    eng.sem_inc(passed, 1)


def ring_before(i):
    return i - RING if i >= RING else [63, 61, 62][i] - UNITS


def stages(T):
    return dict(ln=0 <= T + 3 < ITEMS, proj=0 <= T + 2 < ITEMS, mx=0 <= T + 1 < ITEMS,
                attn=0 <= T < ITEMS, out=0 <= T - 1 < ITEMS, ffn=0 <= T - 2 < ITEMS,
                next_ln=0 <= T + 4 < ITEMS, first_ln=T + 3 == 0, first_proj=T + 2 == 0)


STEADY = dict(ln=True, proj=True, mx=True, attn=True, out=True, ffn=True,
              next_ln=True, first_ln=False, first_proj=False)
HT_SLOT, XT_SLOT, FC1_SLOTS, QK_SLOTS, OUT_SLOT, FC2_SLOTS, V_SLOT = 1, 0, [5, 6, 7, 8], [3, 4], 9, [10, 11], 14
MAXT_SLOTS = [13, 2]
O_SLOTS = [5, 9, 13, 1]
PART_SLOTS = [(0, 0, 7), (1, 0, 9), (1, 1, 10)]
Q_PART2_SLOT = 8
LOOP_FROM, LOOP_TO = 4, 28
FIRST, LAST = -3, ITEMS + 1
TAIL = ITEMS - 3


def run_bodies(eng, body, before={}):
    for T in range(FIRST, LOOP_FROM):
        if T in before:
            before[T]()
        body(T, T % 2, stages(T))
    with eng.Fori(LOOP_FROM // 2, LOOP_TO // 2) as u:
        body(2 * u, 0, STEADY)
        body(2 * u + 1, 1, STEADY)
    for T in range(LOOP_TO, LAST + 1):
        body(T, T % 2, stages(T))


def hybrid_layers(nc, x, w_attn, b_qk, b_v, b_out, gamma, beta, fc1_q, fc1_s, fc1_b, fc2_q, fc2_s, fc2_b,
                  cos_t, sin_t, ident_t, out):
    with ExitStack() as ctx:
        def sb(name, shape, dt=F32):
            return ctx.enter_context(nc.sbuf_tensor(name, shape, dt))

        def ps(name, shape, dt=F32):
            return ctx.enter_context(nc.psum_tensor(name, shape, dt))

        def sem(name):
            return ctx.enter_context(nc.semaphore(name))

        hidden = nc.dram_tensor("hidden", (BATCH, P, R * D), F32, kind="Internal").ap()
        qk_dram = nc.dram_tensor("qk_dram", (2, P, QK_ROWS, TOK), BF16, kind="Internal").ap()
        o_dram = nc.dram_tensor("o_dram", (QUADS, 4, VCOLS, TOK), F32, kind="Internal").ap()
        l_dram = nc.dram_tensor("l_dram", (P, TOK // HD), F32, kind="Internal").ap()

        ident = sb("ident", [P, P])
        ident_bf = sb("ident_bf", [P, P], BF16)
        cos_sb = sb("cos_sb", [P, TOK])
        sin_sb = sb("sin_sb", [P, TOK])
        w_qk = sb("w_qk", [P, 2, D])
        w_v = sb("w_v", [P, D])
        w_out = sb("w_out", [P, D])
        qk_bias = sb("qk_bias", [P, 2])
        v_bias = sb("v_bias", [P, R, D])
        out_bias = sb("out_bias", [P, R, D])
        gamma_sb = sb("gamma_sb", [P, 1])
        beta_sb = sb("beta_sb", [P, 1])
        q1_int = sb("q1_int", [P, FF], I32)
        q2_int = sb("q2_int", [P, FC, D], I32)
        s1 = sb("s1", [P, FF])
        s2 = sb("s2", [P, FC, D])
        w1 = sb("w1", [P, FF])
        w2 = sb("w2", [P, FC, D])
        fc1_bias = sb("fc1_bias", [P, FC])
        fc1_bias_half = sb("fc1_bias_half", [P, FC])
        fc2_bias_in = sb("fc2_bias_in", [P, R, D])
        fc2_bias_half = sb("fc2_bias_half", [P, R, D])
        neg_half = sb("neg_half", [P, R])
        fill = sb("fill", [P, 2, TOK], BF16)

        x_in = sb("x_in", [P, R, D])
        xn = sb("xn", [P, R, D])
        xnT = [sb(f"xnT{i}", [P, TOK]) for i in range(2)]
        lin = [sb("q_lin", [P, TOK]), sb("k_lin", [P, TOK])]
        swapped = [sb("q_swapped", [P, TOK]), sb("k_swapped", [P, TOK])]
        rope_a = sb("rope_a", [P, TOK])
        rope_b = sb("rope_b", [P, TOK])
        rotated = [sb("q_rot", [P, TOK]), sb("k_rot", [P, TOK])]
        rest = [sb("q_rest", [P, TOK]), sb("k_rest", [P, TOK])]
        parts = [sb("q_parts", [P, 3, TOK], BF16), sb("k_parts", [P, 3, TOK], BF16)]
        q_stack = [sb(f"q_stack{i}", [P, HEADS // 2, TOK], BF16) for i in range(2)]
        k_stack = [sb(f"k_stack{i}", [P, HEADS // 2, TOK], BF16) for i in range(2)]
        v_sb = [sb(f"v_sb{i}", [P, R, HEADS, VCOLS]) for i in range(2)]
        neg_max = sb("neg_max", [P, QUADS, R, 2, 2])
        max_parts = sb("max_parts", [P, R, 2, 2, 3, 2], BF16)
        max_rest = sb("max_rest", [P, R, 2, 2])
        max_rows = sb("max_rows", [24, 2, TOK], BF16)
        probs = sb("probs", [P, PBUF, 4, TOK])
        o_sb = sb("o_sb", [P, 2, TOK])
        l_sb = sb("l_sb", [P, TOK // HD])
        l_inv = sb("l_inv", [P, TOK // HD])
        l_bc = sb("l_bc", [P, TOK])
        attn_raw = sb("attn_raw", [P, TOK])
        attnT = sb("attnT", [P, TOK])
        x_res = sb("x_res", [P, R, D])
        x_biased = sb("x_biased", [P, R, D])
        x1 = sb("x1", [P, R, D])
        h0 = sb("h0", [P, R, D])
        hn = sb("hn", [P, R, D])
        hT = sb("hT", [P, TOK])
        fc1_y = sb("fc1_y", [P, 2, TOK])
        fc1_t = sb("fc1_t", [P, 2, TOK])
        act_sb = sb("act_sb", [P, FC, TOK])
        x1_h0 = sb("x1_h0", [P, R, D])
        x2_base = sb("x2_base", [P, R, D])
        x2 = sb("x2", [P, R, D])
        LN_IN, LN_A, LN_B = range(3)
        stats = sb("stats", [P, 3, R, 6])
        mean_var = sb("mean_var", [P, 3, R, 2])
        var_eps = sb("var_eps", [P, 3, R])
        rstd = sb("rstd", [P, 3, R])

        s_bank = [ps(f"s_bank{i}", [P, TOK]) for i in range(RING)]
        t_bank = [ps(f"t_bank{i}", [P, TOK]) for i in range(RING)]
        o_bank = ps("o_bank", [P, TOK])
        misc = ps("misc", [P, TOK])
        misc_bf = misc[:, 0:TOK // 2].bitcast(BF16)

        def exp_bank(i, on):
            return t_bank[i % RING] if on["mx"] else (t_bank + [s_bank[0]])[i % (RING + 1)]

        def tail_fc1_bank(c):
            return s_bank[1 + c % 2]

        ident_loaded = sem("ident_loaded")
        tables_loaded = sem("tables_loaded")
        const_loaded = sem("const_loaded")
        fill_ready = sem("fill_ready")
        fill_written = sem("fill_written")
        dve_setup = sem("dve_setup")
        pool_setup = sem("pool_setup")
        qk_w_loaded = sem("qk_w_loaded")
        v_w_loaded = sem("v_w_loaded")
        out_w_loaded = sem("out_w_loaded")
        qk_w_ok = sem("qk_w_ok")
        v_w_ok = sem("v_w_ok")
        out_w_ok = sem("out_w_ok")
        x_in_loaded = sem("x_in_loaded")
        ln_stat = [sem(f"ln_stat{i}") for i in range(3)]
        ln_rstd = [sem(f"ln_rstd{i}") for i in range(3)]
        ln_norm = [sem(f"ln_norm{i}") for i in range(3)]
        xT_ready = sem("xT_ready")
        xT_copied = sem("xT_copied")
        qk_ready = sem("qk_ready")
        lin_copied = sem("lin_copied")
        swap_done = sem("swap_done")
        rope_done = sem("rope_done")
        rope_sum = sem("rope_sum")
        part_copied = sem("part_copied")
        q_part2_copied = sem("q_part2_copied")
        part_rest = sem("part_rest")
        parts_written = sem("parts_written")
        stack_loaded = [sem(f"stack_loaded{g}") for g in range(QUADS)]
        v_ready = sem("v_ready")
        v_done = sem("v_done")
        s_ready = sem("s_ready")
        s_max = sem("s_max")
        max_split = sem("max_split")
        maxT_ready = sem("maxT_ready")
        maxT_copied = sem("maxT_copied")
        max_rows_loaded = [sem(f"max_rows_loaded{g}") for g in range(QUADS)]
        t_ready = sem("t_ready")
        exp_done = sem("exp_done")
        pv_done = sem("pv_done")
        o_copied = sem("o_copied")
        o_written = [sem(f"o_written{i}") for i in range(2)]
        l_loaded = sem("l_loaded")
        o_loaded = sem("o_loaded")
        l_inverted = sem("l_inverted")
        l_written = sem("l_written")
        l_bc_loaded = sem("l_bc_loaded")
        attn_scaled = sem("attn_scaled")
        x_res_loaded = sem("x_res_loaded")
        x_biased_done = sem("x_biased_done")
        out_ready = sem("out_ready")
        x1_done = sem("x1_done")
        hT_ready = sem("hT_ready")
        hT_copied = sem("hT_copied")
        fc1_ready = sem("fc1_ready")
        fc1_copied = sem("fc1_copied")
        y_done = sem("y_done")
        silu_done = sem("silu_done")
        x2_base_done = sem("x2_base_done")
        fc2_ready = sem("fc2_ready")
        x2_done = sem("x2_done")
        stored = sem("stored")

        sp_passed = sem("sp_passed")
        dve_passed = sem("dve_passed")
        pool_passed = sem("pool_passed")

        block = ctx.enter_context(nc.Block())
        n_tables, n_const = 2, 8

        def normalise(eng, which, dst, src):
            for r in range(R):
                nm = eng.tensor_scalar(dst[:, r, :], src[:, r, :], mean_var[:, which, r, 0:1],
                                       rstd[:, which, r:r + 1], ALU.subtract, ALU.mult)
            nm.then_inc(ln_norm[which], 1)

        def o_copy(eng, copy, b, g):
            eng.wait_ge(pv_done, 16 * b + 4 * (g + 1))
            wait_past(eng, o_written[g % 2], 32 * b + 16 * (g // 2))
            copy(o_sb[:, g % 2, :], o_bank[:, :]).then_inc(o_copied, 1)

        def rotate(eng, side, b):
            n = 4 * b + 2 * side
            eng.wait_ge(lin_copied, 2 * b + side + 1)
            wait_past(eng, rope_sum, 2 * b + side)
            eng.tensor_tensor(rope_a[:, :], lin[side][:, :], cos_sb[:, :], ALU.mult).then_inc(rope_done, 1)
            eng.wait_ge(swap_done, 2 * b + side + 1)
            eng.tensor_tensor(rope_b[:, :], swapped[side][:, :], sin_sb[:, :], ALU.mult).then_inc(rope_done, 1)
            eng.wait_ge(rope_done, n + 2)
            wait_past(eng, part_rest, 4 * (b - 1) + 2 * side + 1)
            eng.tensor_tensor(rotated[side][:, :], rope_a[:, :], rope_b[:, :], ALU.add).then_inc(rope_sum, 1)

        def part_subtract(eng, side, n, b):
            if side == 0 and n == 1:
                eng.wait_ge(q_part2_copied, b + 1)
            else:
                eng.wait_ge(part_copied, 3 * b + side + n + 1)
            if n == 0:
                eng.tensor_tensor(rest[side][:, :], rotated[side][:, :], parts[side][:, 0, :],
                                  ALU.subtract).then_inc(part_rest, 1)
            else:
                eng.tensor_tensor(parts[side][:, 2, :], rest[side][:, :], parts[side][:, 1, :],
                                  ALU.subtract).then_inc(part_rest, 1)

        @block.sync
        def _(sp):
            def load_qk_weights(layer):
                sp.dma_start(w_qk[:, :, :], w_attn[layer, :, 0:2, :]).then_inc(qk_w_loaded, 16)
                sp.dma_start(qk_bias[:, :], b_qk[layer]).then_inc(qk_w_loaded, 16)

            def load_v_weights(layer):
                sp.dma_start(w_v[:, :], w_attn[layer, :, 2, :]).then_inc(v_w_loaded, 16)
                sp.dma_start(v_bias[:, :, :], per_row(b_v[layer:layer + 1])).then_inc(v_w_loaded, 16)

            def load_out_weights(layer):
                sp.dma_start(w_out[:, :], w_attn[layer, :, 3, :]).then_inc(out_w_loaded, 16)
                sp.dma_start(out_bias[:, :, :], per_row(b_out[layer:layer + 1])).then_inc(out_w_loaded, 16)

            def rows_of(b, layer):
                return x[b] if layer == 0 else hidden[b - BATCH]

            def max_rows_in(b, par, pair):
                sp.wait_ge(maxT_copied, 2 * b + pair + 1)
                for g in (2 * pair, 2 * pair + 1):
                    for s in range(2):
                        sp.dma_start(q_stack[par][64 * s + MAX_ROW:64 * s + MAX_ROW + 3 * HD:HD, 2 * g:2 * g + 2, :],
                                     max_rows[12 * (g % 2) + 6 * s:12 * (g % 2) + 6 * s + 6, pair, :])\
                            .then_inc(max_rows_loaded[g], 16)

            def o_out(b, g):
                if g == 0:
                    wait_past(sp, l_loaded, 16 * b)
                    wait_past(sp, o_loaded, 16 * b)
                sp.wait_ge(o_copied, 4 * b + g + 1)
                sp.dma_start(o_dram[g].rearrange("j c n -> (j c) n"), o_sb[:, g % 2, :]).then_inc(o_written[g % 2], 16)

            def stack_in(b, par, g):
                wait_past(sp, t_ready, UNITS * (b - 2) + 16 * (g + 1))
                for side, dst in ((0, q_stack[par]), (1, k_stack[par])):
                    src = qk_dram[side].rearrange("(p s d) t n -> p (s d t) n", s=2, d=HD)
                    sp.dma_start(dst[:, 2 * g:2 * g + 2, :],
                                 src[2 * g:2 * g + 2].rearrange("p r n -> r p n")).then_inc(stack_loaded[g], 16)

            def body(T, par, on, in_layer=0, res_layer=0, store_layer=0, reload_qk=False, reload_v=False,
                     reload_out=False):
                if on["proj"]:
                    if reload_qk:
                        sp.wait_ge(lin_copied, 2 * BATCH)
                        load_qk_weights(1)
                        sp.wait_ge(qk_w_loaded, 64)
                    sp.sem_inc(qk_w_ok, 1)
                    if on["first_proj"]:
                        sp.wait_ge(fill_ready, 2)
                        for s in range(2):
                            sp.dma_start(qk_dram[s, :, MAX_ROW, :], fill[:, s, :]).then_inc(fill_written, 16)
                        load_v_weights(0)
                        load_out_weights(0)
                if on["mx"]:
                    if reload_v:
                        sp.wait_ge(v_done, BATCH)
                        load_v_weights(1)
                        sp.wait_ge(v_w_loaded, 64)
                    sp.sem_inc(v_w_ok, 1)
                if on["out"]:
                    b = T - 1
                    o_out(b, 3)
                    for i in range(2):
                        sp.wait_ge(o_written[i], 32 * (b + 1))
                    pass_alone(sp, sp_passed)
                    wait_past(sp, l_inverted, b)
                    sp.dma_start(l_sb[:, :], o_dram[:, :, HD, :].rearrange("g j (a n) -> (g j) a n", a=HD))\
                        .then_inc(l_loaded, 16)
                    wait_past(sp, attn_scaled, b)
                    sp.dma_start(attn_raw[:, :], o_dram[:, :, 0:HD, :].rearrange("g j d n -> (g j) d n"))\
                        .then_inc(o_loaded, 16)
                if on["attn"]:
                    wait_past(sp, x_biased_done, T)
                    if res_layer:
                        sp.wait_ge(stored, 16 * (T - BATCH + 1))
                    pass_alone(sp, sp_passed)
                    sp.dma_start(x_res[:, :, :].rearrange("p r d -> p (r d)"), rows_of(T, res_layer)).then_inc(x_res_loaded, 16)
                if on["attn"]:
                    max_rows_in(T, par, 1)
                if on["out"]:
                    b = T - 1
                    sp.wait_ge(l_inverted, b + 1)
                    wait_past(sp, l_bc_loaded, 16 * b)
                    sp.dma_start(l_dram, l_inv[:, :]).then_inc(l_written, 16)
                    sp.wait_ge(l_written, 16 * (b + 1))
                    sp.dma_start(l_bc[:, :], l_dram.rearrange("(h a) (o n) -> h o (a n)", a=HD, o=1)
                                 .to_broadcast([HEADS, HD, TOK])).then_inc(l_bc_loaded, 16)
                if on["attn"]:
                    o_out(T, 0)
                if on["proj"]:
                    b = T + 2
                    for g in range(QUADS):
                        wait_past(sp, stack_loaded[g], 32 * b)
                    sp.wait_ge(part_rest, 4 * b + 2)
                    qp, kp = parts
                    for n, t, m in ((0, 0, 3), (1, 3, 3), (2, 6, 1)):
                        sp.dma_start(qk_dram[0, :, t:t + m, :], qp[:, n:n + 1, :].to_broadcast([P, m, TOK]))\
                            .then_inc(parts_written, 16)
                if on["attn"]:
                    o_out(T, 1)
                if on["proj"]:
                    b = T + 2
                    sp.wait_ge(part_rest, 4 * b + 4)
                    sp.dma_start(qk_dram[1, :, 0:3, :], kp[:, :, :]).then_inc(parts_written, 16)
                    sp.dma_start(qk_dram[1, :, 3:6, :], kp[:, :, :]).then_inc(parts_written, 16)
                    sp.dma_start(qk_dram[1, :, 6, :], kp[:, 0, :]).then_inc(parts_written, 16)
                if on["ffn"]:
                    b = T - 2
                    sp.wait_ge(x2_done, b + 1)
                    pass_alone(sp, sp_passed)
                    dst = hidden[b] if store_layer == 0 else out[b - BATCH]
                    sp.dma_start(dst, x2[:, :, :].rearrange("p r d -> p (r d)")).then_inc(stored, 16)
                if on["proj"]:
                    b = T + 2
                    if on["first_proj"]:
                        sp.wait_ge(fill_written, 32)
                    sp.wait_ge(parts_written, 96 * (b + 1))
                    stack_in(b, par, 0)
                    stack_in(b, par, 1)
                if on["attn"]:
                    o_out(T, 2)
                if on["mx"]:
                    max_rows_in(T + 1, 1 - par, 0)
                if on["attn"]:
                    if reload_out:
                        sp.wait_ge(out_ready, BATCH)
                        sp.wait_ge(x_biased_done, BATCH)
                        load_out_weights(1)
                        sp.wait_ge(out_w_loaded, 64)
                    sp.sem_inc(out_w_ok, 1)
                if on["next_ln"]:
                    b = T + 4
                    wait_past(sp, ln_norm[LN_IN], b)
                    if in_layer:
                        sp.wait_ge(stored, 16 * (b - BATCH + 1))
                    pass_alone(sp, sp_passed)
                    sp.dma_start(x_in[:, :, :].rearrange("p r d -> p (r d)"), rows_of(b, in_layer)).then_inc(x_in_loaded, 16)
                if on["proj"]:
                    stack_in(T + 2, par, 2)
                    stack_in(T + 2, par, 3)

            def single(T):
                body(T, T % 2, stages(T), in_layer=int(T + 4 >= BATCH), res_layer=int(T >= BATCH),
                     store_layer=int(T - 2 >= BATCH), reload_qk=T + 2 == BATCH, reload_v=T + 1 == BATCH,
                     reload_out=T == BATCH)

            sp.dma_start(x_in[:, :, :].rearrange("p r d -> p (r d)"), rows_of(0, 0)).then_inc(x_in_loaded, 16)
            sp.dma_start(ident[:, :], ident_t).then_inc(ident_loaded, 16)
            load_qk_weights(0)
            for dst, src in ((cos_sb, cos_t), (sin_sb, sin_t)):
                sp.dma_start(dst[:, :], src).then_inc(tables_loaded, 16)
            sp.wait_ge(qk_w_loaded, 32)
            single(FIRST)
            single(FIRST + 1)
            sp.wait_ge(v_w_loaded, 32)
            sp.wait_ge(out_w_loaded, 32)
            for T in range(FIRST + 2, LOOP_FROM):
                single(T)
            with sp.Fori(LOOP_FROM // 2, 6) as u:
                body(2 * u, 0, STEADY)
                body(2 * u + 1, 1, STEADY)
            for T in range(12, BATCH + 2):
                single(T)
            with sp.Fori(BATCH // 2 + 1, LOOP_TO // 2) as u:
                body(2 * u, 0, STEADY, 1, 1, 1)
                body(2 * u + 1, 1, STEADY, 1, 1, 1)
            for T in range(LOOP_TO, LAST + 1):
                single(T)
            sp.wait_ge(stored, 16 * ITEMS)

        @block.tensor
        def _(pe):
            last_misc = [None]

            def misc_free():
                if last_misc[0] is not None:
                    wait_past(pe, *last_misc[0])

            def body(T, par, on):
                def score_max_pair(g, qt, a):
                    b = T + 1
                    if qt == 0 and a == 0:
                        pe.wait_ge(stack_loaded[g], 32 * (b + 1))
                    for s in range(2):
                        i = 16 * g + 4 * qt + 2 * a + s
                        wait_past(pe, s_max, UNITS * b + ring_before(i) + 1)
                        rows = slice(64 * s, 64 * s + 64)
                        nc.tensor.matmul(s_bank[i % RING][:, :], q_stack[1 - par][rows, 2 * g + a, qt * P:(qt + 1) * P],
                                         k_stack[1 - par][rows, 2 * g + a, :], start=True, stop=True).then_inc(s_ready, 1)

                def score_exp_pair(g, kc, a):
                    b = T
                    if kc == 0 and a == 0:
                        pe.wait_ge(max_rows_loaded[g], 32 * (b + 1))
                    for s in range(2):
                        i = 16 * g + 4 * kc + 2 * a + s
                        if on["mx"] or i < RING:
                            wait_past(pe, exp_done, UNITS * b + ring_before(i) + 1)
                        elif i == RING:
                            pe.wait_ge(s_max, UNITS * ITEMS)
                        else:
                            pe.wait_ge(exp_done, UNITS * b + i - RING)
                        rows = slice(64 * s, 64 * s + 64)
                        nc.tensor.matmul(exp_bank(i, on)[:, :], k_stack[par][rows, 2 * g + a, kc * P:(kc + 1) * P],
                                         q_stack[par][rows, 2 * g + a, :], start=True, stop=True).then_inc(t_ready, 1)

                def weighted_sum(b, vpar, k):
                    g, kc = divmod(k, R)
                    if k == 0:
                        pe.wait_ge(v_done, b + 1)
                    if kc == 0:
                        wait_past(pe, o_copied, 4 * b + g)
                    pe.wait_ge(exp_done, UNITS * b + 4 * (k + 1))
                    for j in range(4):
                        mm = nc.tensor.matmul(o_bank[32 * j:32 * j + 32, :], v_sb[vpar][:, kc, 4 * g + j, :],
                                              probs[:, k % PBUF, j, :], start=kc == 0, stop=kc == R - 1)
                    mm.then_inc(pv_done, 1)

                def transpose_rows(src, b, normed, ready, copied):
                    pe.wait_ge(normed, b + 1)
                    misc_free()
                    for r in range(R):
                        mm = nc.tensor.transpose(misc[:, r * P:(r + 1) * P], src[:, r, :], ident[:, :])
                    mm.then_inc(ready, 1)
                    last_misc[0] = (copied, b + 1)

                def project_qk(n):
                    b = T + 2
                    if n == 0:
                        pe.wait_ge(qk_w_ok, b + 1)
                        pe.wait_ge(xT_copied, b + 1)
                    misc_free()
                    nc.tensor.matmul(misc[:, :], w_qk[:, n, :], xnT[par][:, :], start=True, stop=True).then_inc(qk_ready, 1)
                    last_misc[0] = (lin_copied, 2 * b + n + 1)

                def project_v():
                    b = T + 1
                    pe.wait_ge(v_w_ok, b + 1)
                    misc_free()
                    for r in range(R):
                        mm = nc.tensor.matmul(misc[:, r * P:(r + 1) * P], xnT[1 - par][:, r * P:(r + 1) * P], w_v[:, :],
                                              start=True, stop=True)
                    mm.then_inc(v_ready, 1)
                    last_misc[0] = (v_done, b + 1)

                def max_to_rows(b, pair):
                    pe.wait_ge(max_split, 16 * b + 8 * (pair + 1))
                    misc_free()
                    for r in range(R):
                        mm = nc.tensor.transpose(misc_bf[0:24, r * P:(r + 1) * P],
                                                 max_parts[:, r, :, :, :, :].rearrange("p h s n a -> p (h s n a)"),
                                                 ident_bf[:, :])
                    mm.then_inc(maxT_ready, 1)
                    last_misc[0] = (maxT_copied, 2 * b + pair + 1)

                def project_out():
                    b = T - 1
                    pe.wait_ge(attn_scaled, b + 1)
                    pe.wait_ge(out_w_ok, b + 1)
                    misc_free()
                    for r in range(R):
                        mm = nc.tensor.matmul(misc[:, r * P:(r + 1) * P], attnT[:, r * P:(r + 1) * P], w_out[:, :],
                                              start=True, stop=True)
                    mm.then_inc(out_ready, 1)
                    last_misc[0] = (x1_done, b + 1)

                def fc1(c):
                    b = T - 2
                    if c == 0:
                        pe.wait_ge(hT_copied, b + 1)
                    if on["mx"]:
                        bank = misc
                        misc_free()
                        last_misc[0] = (fc1_copied, 4 * b + c + 1)
                    else:
                        bank = tail_fc1_bank(c)
                        pe.wait_ge(s_max, UNITS * ITEMS)
                        wait_past(pe, y_done, 4 * (b - TAIL) + c + 1 - 2)
                    nc.tensor.matmul(bank[:, :], w1[:, c * P:(c + 1) * P], hT[:, :], start=True, stop=True).then_inc(fc1_ready, 1)

                def fc2(r):
                    b = T - 2
                    if r == 0:
                        pe.wait_ge(silu_done, 4 * (b + 1))
                        misc_free()
                    for c in range(FC):
                        mm = nc.tensor.matmul(misc[:, r * P:(r + 1) * P], act_sb[:, c, r * P:(r + 1) * P], w2[:, c, :],
                                              start=c == 0, stop=c == FC - 1)
                    if r == R - 1:
                        mm.then_inc(fc2_ready, 1)
                        last_misc[0] = (x2_done, b + 1)

                if not isinstance(T, int) or T == LOOP_TO:
                    last_misc[0] = (v_done, T + 1)
                for k in range(SLOTS):
                    g, n = divmod(k, R)
                    if on["attn"]:
                        score_exp_pair(g, n, 0)
                    if on["mx"]:
                        score_max_pair(g, n, 0)
                    if k == HT_SLOT and on["ffn"]:
                        transpose_rows(hn, T - 2, ln_norm[LN_B], hT_ready, hT_copied)
                    if k == XT_SLOT and on["proj"]:
                        transpose_rows(xn, T + 2, ln_norm[LN_IN], xT_ready, xT_copied)
                    if k in FC1_SLOTS and on["ffn"]:
                        fc1(FC1_SLOTS.index(k))
                    if k in QK_SLOTS and on["proj"]:
                        project_qk(QK_SLOTS.index(k))
                    if k == OUT_SLOT and on["out"]:
                        project_out()
                    if k in FC2_SLOTS and on["ffn"]:
                        fc2(2 * FC2_SLOTS.index(k))
                    if k == V_SLOT and on["mx"]:
                        project_v()
                    if k == MAXT_SLOTS[1] and on["attn"]:
                        max_to_rows(T, 1)
                    if k == MAXT_SLOTS[0] and on["mx"]:
                        max_to_rows(T + 1, 0)
                    if on["attn"]:
                        score_exp_pair(g, n, 1)
                    if on["mx"]:
                        score_max_pair(g, n, 1)
                    if k in FC2_SLOTS and on["ffn"]:
                        fc2(2 * FC2_SLOTS.index(k) + 1)
                    if k == 0 and on["out"]:
                        weighted_sum(T - 1, 1 - par, SLOTS - 1)
                    if k > 0 and on["attn"]:
                        weighted_sum(T, par, k - 1)

            run_bodies(pe, body, {FIRST + 1: lambda: pe.wait_ge(ident_loaded, 16),
                                  FIRST + 2: lambda: pe.wait_ge(dve_setup, 4)})

        @block.scalar
        def _(act):
            for dst, src in (
                (q1_int[:, :], fc1_q), (s1[:, :], fc1_s.to_broadcast([P, FF])),
                (q2_int[:, :, :], fc2_q.rearrange("(c p) n -> p c n", p=P)),
                (s2[:, :, :].rearrange("p c n -> p (c n)"), fc2_s.to_broadcast([P, FF])),
                (gamma_sb[:, :], gamma), (beta_sb[:, :], beta), (fc1_bias[:, :], fc1_b),
                (fc2_bias_in[:, :, :], per_row(fc2_b)),
            ):
                act.dma_start(dst, src).then_inc(const_loaded, 16)

            def body(T, par, on):
                def exps(k, a):
                    if a == 0:
                        wait_past(act, pv_done, 16 * T + k + 1 - PBUF)
                    for s in range(2):
                        i = 4 * k + 2 * a + s
                        act.wait_ge(t_ready, UNITS * T + i + 1)
                        nc.scalar.activation(probs[:, k % PBUF, 2 * a + s, :], exp_bank(i, on)[:, :], ACT.Exp,
                                             scale=SCALE).then_inc(exp_done, 1)

                def max_rows_copy(b, pair):
                    act.wait_ge(maxT_ready, 2 * b + pair + 1)
                    for g in (2 * pair, 2 * pair + 1):
                        wait_past(act, max_rows_loaded[g], 32 * b)
                    nc.scalar.copy(max_rows[:, pair, :], misc_bf[0:24, :]).then_inc(maxT_copied, 1)

                def part_copy(side, n):
                    b = T + 2
                    if side == 0 and n == 0:
                        wait_past(act, parts_written, 96 * b)
                    if n == 0:
                        act.wait_ge(rope_sum, 2 * b + side + 1)
                    else:
                        act.wait_ge(part_rest, 4 * b + 3)
                    src = rotated[side] if n == 0 else rest[side]
                    nc.scalar.copy(parts[side][:, n, :], src[:, :]).then_inc(part_copied, 1)

                def add_bias(side):
                    b = T + 2
                    act.wait_ge(qk_ready, 2 * b + side + 1)
                    wait_past(act, rope_done, 4 * (b - 1) + 2 * side + 2)
                    nc.scalar.activation(lin[side][:, :], misc[:, :], ACT.Identity,
                                         bias=qk_bias[:, side:side + 1]).then_inc(lin_copied, 1)

                def silu_terms(c):
                    b = T - 2
                    wait_past(act, silu_done, 4 * b + c - 1)
                    if on["mx"]:
                        act.wait_ge(fc1_ready, 4 * b + c + 1)
                        nc.scalar.activation(fc1_y[:, c % 2, :], misc[:, :], ACT.Identity, bias=fc1_bias[:, c:c + 1])
                        nc.scalar.activation(fc1_t[:, c % 2, :], misc[:, :], ACT.Tanh, bias=fc1_bias_half[:, c:c + 1],
                                             scale=0.5).then_inc(fc1_copied, 1)
                    else:
                        act.wait_ge(y_done, 4 * (b - TAIL) + c + 1)
                        nc.scalar.activation(fc1_t[:, c % 2, :], fc1_y[:, c % 2, :], ACT.Tanh,
                                             scale=0.5).then_inc(fc1_copied, 1)

                for k in range(SLOTS):
                    if on["attn"]:
                        exps(k, 0)
                    if k == O_SLOTS[3] and on["out"] and on["mx"]:
                        o_copy(act, nc.scalar.copy, T - 1, 3)
                    if k in O_SLOTS[0:3] and on["attn"] and on["mx"]:
                        o_copy(act, nc.scalar.copy, T, O_SLOTS.index(k))
                    for side, n, slot in PART_SLOTS:
                        if k == slot and on["proj"]:
                            part_copy(side, n)
                    if k in FC1_SLOTS and on["ffn"]:
                        silu_terms(FC1_SLOTS.index(k))
                    if k == XT_SLOT and on["proj"]:
                        b = T + 2
                        act.wait_ge(xT_ready, b + 1)
                        wait_past(act, v_ready, b - 1)
                        nc.scalar.copy(xnT[par][:, :], misc[:, :]).then_inc(xT_copied, 1)
                    if k in QK_SLOTS and on["proj"]:
                        add_bias(QK_SLOTS.index(k))
                    if k == HT_SLOT and on["ffn"]:
                        b = T - 2
                        act.wait_ge(hT_ready, b + 1)
                        wait_past(act, fc1_ready, 4 * b)
                        nc.scalar.activation(hT[:, :], misc[:, :], ACT.Identity, bias=beta_sb[:, 0:1],
                                             scale=gamma_sb[:, 0:1]).then_inc(hT_copied, 1)
                    if k == MAXT_SLOTS[1] and on["attn"]:
                        max_rows_copy(T, 1)
                    if k == MAXT_SLOTS[0] and on["mx"]:
                        max_rows_copy(T + 1, 0)
                    if on["attn"]:
                        exps(k, 1)

            run_bodies(act, body, {FIRST + 2: lambda: act.wait_ge(dve_setup, 4)})

        @block.vector
        def _(dve):
            nc.vector.memset(fill[:, 0, :], 0.0).then_inc(fill_ready, 1)
            nc.vector.memset(fill[:, 1, :], 1.0).then_inc(fill_ready, 1)

            def prepare():
                dve.wait_ge(pool_setup, 5)
                dve.wait_ge(ident_loaded, 16)
                nc.vector.tensor_copy(ident_bf[:, :], ident[:, :])
                dve.wait_ge(const_loaded, 16 * n_const)
                nc.vector.scalar_tensor_tensor(out=w1[:, :], in0=q1_int[:, :], scalar=-128.0, in1=s1[:, :],
                                               op0=ALU.add, op1=ALU.mult).then_inc(dve_setup, 1)
                nc.vector.scalar_tensor_tensor(out=w2[:, :, :], in0=q2_int[:, :, :], scalar=-128.0, in1=s2[:, :, :],
                                               op0=ALU.add, op1=ALU.mult).then_inc(dve_setup, 1)
                dve.wait_ge(dve_setup, 2)
                nc.vector.tensor_scalar(w2[:, :, :], w2[:, :, :], 0.25, None, ALU.mult).then_inc(dve_setup, 1)
                nc.vector.tensor_scalar(fc1_bias_half[:, :], fc1_bias[:, :], 0.5, None, ALU.mult)
                nc.vector.tensor_scalar(fc2_bias_half[:, :, :], fc2_bias_in[:, :, :], 0.5, None,
                                        ALU.mult).then_inc(dve_setup, 1)

            def layer_norm_stats(which, src, b):
                for r in range(R):
                    st = nc.vector.bn_stats(stats[:, which, r, :], src[:, r, :])
                st.then_inc(ln_stat[which], 1)

            def layer_norm_variance(which, b):
                dve.wait_ge(ln_stat[which], 3 * b + 1)
                pass_alone(dve, dve_passed)
                for r in range(R):
                    ag = nc.vector.bn_aggr(mean_var[:, which, r, :], stats[:, which, r, :])
                ag.then_inc(ln_stat[which], 1)
                dve.wait_ge(ln_stat[which], 3 * b + 2)
                nc.vector.tensor_scalar(var_eps[:, which, :], mean_var[:, which, :, 1], EPS, None, ALU.add)\
                    .then_inc(ln_stat[which], 1)

            def layer_norm_apply(which, dst, src, b):
                dve.wait_ge(ln_rstd[which], b + 1)
                normalise(dve, which, dst, src)

            def body(T, par, on):
                def maxima(k, a):
                    b = T + 1
                    g, qt = divmod(k, R)
                    if qt == 0 and a == 0:
                        wait_past(dve, max_split, 16 * (b - 1) + 4 * g + 2)
                    for s in range(2):
                        i = 4 * k + 2 * a + s
                        dve.wait_ge(s_ready, UNITS * b + i + 1)
                        nc.vector.tensor_reduce(neg_max[:, g, qt, s, a:a + 1], s_bank[i % RING][:, :], AX_X, ALU.max,
                                                negate=True).then_inc(s_max, 1)

                def swap_halves(side):
                    b = T + 2
                    wait_past(dve, rope_done, 4 * (b - 1) + 2 * side + 2)
                    dve.wait_ge(lin_copied, 2 * b + side + 1)
                    pass_alone(dve, dve_passed)
                    nc.vector.stream_shuffle(swapped[side][:, :], lin[side][:, :], HALVES_SWAPPED).then_inc(swap_done, 1)

                def silu(c):
                    b = T - 2
                    dve.wait_ge(fc1_copied, 4 * b + c + 1)
                    if c == 0:
                        wait_past(dve, fc2_ready, b)
                    nc.vector.scalar_tensor_tensor(out=act_sb[:, c, :], in0=fc1_t[:, c % 2, :], scalar=1.0,
                                                   in1=fc1_y[:, c % 2, :], op0=ALU.add, op1=ALU.mult).then_inc(silu_done, 1)

                for k in range(SLOTS):
                    if on["mx"]:
                        maxima(k, 0)
                    if k == O_SLOTS[3] and on["out"] and not on["mx"]:
                        o_copy(dve, nc.vector.tensor_copy, T - 1, 3)
                    if k in O_SLOTS[0:3] and on["attn"] and not on["mx"]:
                        o_copy(dve, nc.vector.tensor_copy, T, O_SLOTS.index(k))
                    if k in FC1_SLOTS and on["ffn"] and not on["mx"]:
                        b, c = T - 2, FC1_SLOTS.index(k)
                        dve.wait_ge(fc1_ready, 4 * b + c + 1)
                        dve.wait_ge(silu_done, 4 * b + c - 1)
                        nc.vector.tensor_scalar(fc1_y[:, c % 2, :], tail_fc1_bank(c)[:, :],
                                                fc1_bias[:, c:c + 1], None, ALU.add).then_inc(y_done, 1)
                    if k == 0 and on["ffn"] and not on["attn"]:
                        wait_past(dve, hT_ready, T - 2)
                        layer_norm_apply(LN_B, hn, h0, T - 2)
                    if k == 1 and on["ln"]:
                        dve.wait_ge(x_in_loaded, 16 * (T + 4))
                        layer_norm_stats(LN_IN, x_in, T + 3)
                    if k == 2 and on["ln"]:
                        layer_norm_variance(LN_IN, T + 3)
                        if on["first_ln"]:
                            layer_norm_apply(LN_IN, xn, x_in, 0)
                    if k - 1 in QK_SLOTS and on["proj"]:
                        swap_halves(QK_SLOTS.index(k - 1))
                        if on["first_proj"]:
                            rotate(dve, QK_SLOTS.index(k - 1), 0)
                    if k == 4 and on["out"]:
                        b = T - 1
                        dve.wait_ge(l_loaded, 16 * (b + 1))
                        wait_past(dve, l_written, 16 * b)
                        nc.vector.reciprocal(l_inv[:, :], l_sb[:, :]).then_inc(l_inverted, 1)
                    if k - 1 in FC1_SLOTS and on["ffn"]:
                        silu(FC1_SLOTS.index(k - 1))
                    if k == Q_PART2_SLOT and on["first_proj"]:
                        part_subtract(dve, 0, 0, 0)
                    if k == Q_PART2_SLOT and on["proj"]:
                        b = T + 2
                        dve.wait_ge(part_rest, 4 * b + 1)
                        wait_past(dve, parts_written, 96 * b)
                        nc.vector.tensor_copy(parts[0][:, 1, :], rest[0][:, :]).then_inc(q_part2_copied, 1)
                    if k == Q_PART2_SLOT and on["first_proj"]:
                        part_subtract(dve, 0, 1, 0)
                        part_subtract(dve, 1, 0, 0)
                        part_subtract(dve, 1, 1, 0)
                    if k == OUT_SLOT and on["out"]:
                        b = T - 1
                        dve.wait_ge(out_ready, b + 1)
                        dve.wait_ge(x_biased_done, b + 1)
                        wait_past(dve, x2_base_done, 2 * b)
                        nc.vector.tensor_tensor(x1[:, :, :].rearrange("p r d -> p (r d)"), misc[:, :],
                                                x_biased[:, :, :].rearrange("p r d -> p (r d)"), ALU.add).then_inc(x1_done, 1)
                    if k == OUT_SLOT + 1 and on["out"]:
                        dve.wait_ge(x1_done, T)
                        layer_norm_stats(LN_A, x1, T - 1)
                        layer_norm_variance(LN_A, T - 1)
                    if k == OUT_SLOT + 2 and on["out"]:
                        layer_norm_apply(LN_A, h0, x1, T - 1)
                    if k == FC2_SLOTS[-1] + 1 and on["ffn"]:
                        b = T - 2
                        dve.wait_ge(fc2_ready, b + 1)
                        dve.wait_ge(x2_base_done, 2 * (b + 1))
                        wait_past(dve, stored, 16 * b)
                        nc.vector.tensor_tensor(x2[:, :, :].rearrange("p r d -> p (r d)"), misc[:, :],
                                                x2_base[:, :, :].rearrange("p r d -> p (r d)"), ALU.add).then_inc(x2_done, 1)
                    if k == OUT_SLOT + 4 and on["out"]:
                        layer_norm_variance(LN_B, T - 1)
                    if k == V_SLOT and on["mx"]:
                        b = T + 1
                        dve.wait_ge(v_ready, b + 1)
                        wait_past(dve, pv_done, 16 * (b - 1))
                        nc.vector.tensor_tensor(v_sb[1 - par][:, :, :, 0:HD].rearrange("p r h d -> p (r h) d"),
                                                misc[:, :].rearrange("p (m d) -> p m d", d=HD),
                                                v_bias[:, :, :].rearrange("p r (h d) -> p (r h) d", d=HD),
                                                ALU.add).then_inc(v_done, 1)
                    if on["mx"]:
                        maxima(k, 1)
                    if k == OUT_SLOT + 2 and on["out"]:
                        dve.wait_ge(ln_norm[LN_A], T)
                        layer_norm_stats(LN_B, h0, T - 1)

            run_bodies(dve, body, {FIRST + 1: lambda: dve.wait_ge(tables_loaded, 16 * n_tables), FIRST + 2: prepare})

        @block.gpsimd
        def _(pool):
            nc.gpsimd.memset(neg_half[:, :], -0.5).then_inc(pool_setup, 1)
            pool.wait_ge(pool_setup, 1)

            def fix_v_columns():
                for i in range(2):
                    nc.gpsimd.memset(v_sb[i][:, :, :, :], 0.0).then_inc(pool_setup, 1)
                pool.wait_ge(pool_setup, 3)
                for i in range(2):
                    nc.gpsimd.memset(v_sb[i][:, :, :, HD:HD + 1], 1.0).then_inc(pool_setup, 1)
                pool.wait_ge(tables_loaded, 16 * n_tables)

            def inverse_deviation(which, b):
                pool.wait_ge(ln_stat[which], 3 * (b + 1))
                nc.gpsimd.tensor_tensor(rstd[:, which, :], var_eps[:, which, :], neg_half[:, :], ALU.pow)\
                    .then_inc(ln_rstd[which], 1)

            def split_max(b, g):
                n = 16 * b + 4 * g
                pool.wait_ge(s_max, UNITS * b + 16 * (g + 1))
                wait_past(pool, maxT_ready, 2 * b + g // 2)
                pass_alone(pool, pool_passed)
                nc.gpsimd.tensor_copy(max_parts[:, :, g % 2, :, 0, :], neg_max[:, g, :, :, :]).then_inc(max_split, 1)
                pool.wait_ge(max_split, n + 1)
                nc.gpsimd.tensor_tensor(max_rest[:, :, :, :], neg_max[:, g, :, :, :], max_parts[:, :, g % 2, :, 0, :],
                                        ALU.subtract).then_inc(max_split, 1)
                pool.wait_ge(max_split, n + 2)
                pass_alone(pool, pool_passed)
                nc.gpsimd.tensor_copy(max_parts[:, :, g % 2, :, 1, :], max_rest[:, :, :, :]).then_inc(max_split, 1)
                pool.wait_ge(max_split, n + 3)
                nc.gpsimd.tensor_tensor(max_parts[:, :, g % 2, :, 2, :], max_rest[:, :, :, :], max_parts[:, :, g % 2, :, 1, :],
                                        ALU.subtract).then_inc(max_split, 1)

            def flat(t):
                return t[:, :, :].rearrange("p r d -> p (r d)")

            def body(T, par, on):
                if on["attn"]:
                    split_max(T, 3)
                if on["out"]:
                    b = T - 1
                    pool.wait_ge(x_res_loaded, 16 * (b + 1))
                    pool.wait_ge(out_w_ok, b + 1)
                    wait_past(pool, x1_done, b)
                    nc.gpsimd.tensor_tensor(flat(x_biased), flat(x_res), flat(out_bias), ALU.add).then_inc(x_biased_done, 1)
                if on["ln"]:
                    b = T + 3
                    inverse_deviation(LN_IN, b)
                if on["ln"] and not on["first_ln"]:
                    wait_past(pool, xT_ready, b)
                    pool.wait_ge(ln_rstd[LN_IN], b + 1)
                    pass_alone(pool, pool_passed)
                    normalise(pool, LN_IN, xn, x_in)
                if on["mx"]:
                    split_max(T + 1, 0)
                if on["proj"] and not on["first_proj"]:
                    rotate(pool, 0, T + 2)
                    rotate(pool, 1, T + 2)
                if on["out"]:
                    b = T - 1
                    pool.wait_ge(o_loaded, 16 * (b + 1))
                    pool.wait_ge(l_bc_loaded, 16 * (b + 1))
                    wait_past(pool, out_ready, b)
                    nc.gpsimd.tensor_tensor(attnT[:, :], attn_raw[:, :], l_bc[:, :], ALU.mult).then_inc(attn_scaled, 1)
                if on["proj"] and not on["first_proj"]:
                    part_subtract(pool, 0, 0, T + 2)
                if on["mx"]:
                    split_max(T + 1, 1)
                if on["proj"] and not on["first_proj"]:
                    part_subtract(pool, 0, 1, T + 2)
                    part_subtract(pool, 1, 0, T + 2)
                if on["out"]:
                    inverse_deviation(LN_A, T - 1)
                if on["proj"] and not on["first_proj"]:
                    part_subtract(pool, 1, 1, T + 2)
                if on["out"]:
                    b = T - 1
                    pool.wait_ge(ln_norm[LN_A], b + 1)
                    nc.gpsimd.tensor_tensor(flat(x1_h0), flat(x1), flat(h0), ALU.add).then_inc(x2_base_done, 1)
                    pool.wait_ge(x2_base_done, 2 * b + 1)
                    wait_past(pool, x2_done, b)
                    nc.gpsimd.tensor_tensor(flat(x2_base), flat(x1_h0), flat(fc2_bias_half), ALU.add).then_inc(x2_base_done, 1)
                if on["mx"]:
                    split_max(T + 1, 2)
                if on["out"]:
                    inverse_deviation(LN_B, T - 1)
                if on["out"] and on["mx"]:
                    b = T - 1
                    wait_past(pool, hT_ready, b)
                    pool.wait_ge(ln_rstd[LN_B], b + 1)
                    pass_alone(pool, pool_passed)
                    normalise(pool, LN_B, hn, h0)

            run_bodies(pool, body, {FIRST + 1: fix_v_columns,
                                    FIRST + 2: lambda: pool.wait_ge(dve_setup, 4)})


def kernel(**inputs):
    import numpy as np
    from concourse import bacc
    from concourse.bass_utils import run_bass_kernel_spmd

    a = {n: np.asarray(v) for n, v in inputs.items()}

    even, odd = np.arange(0, HD, 2), np.arange(1, HD, 2)
    cols = (np.arange(HEADS)[:, None] * HD + np.concatenate([even, odd])[None]).ravel()
    w_attn, b_qk, b_v, b_out = [], [], [], []
    for n in ("L0_attn_a", "L0_attn_b"):
        w, wo, b = a[f"{n}_qkv_w"], a[f"{n}_out_w"], a[f"{n}_qkv_b"]
        q, k, v = w[:, 0:D], w[:, D:2 * D], w[:, 2 * D:3 * D]
        w_attn.append(np.stack([q[:, cols], k[:, cols], v, wo], axis=1))
        b_qk.append(np.stack([b[0:D][cols], b[D:2 * D][cols]], axis=1))
        b_v.append(b[2 * D:3 * D])
        b_out.append(a[f"{n}_out_b"])

    freqs = (np.float32(10000.0) ** (np.arange(0, HD, 2.0, dtype=np.float32) / HD)).astype(np.float32)
    angles = np.arange(TOK, dtype=np.float32)[:, None] * freqs[None, :]
    order = (np.arange(P)[None, :] * R + np.arange(R)[:, None]).ravel()
    cos, sin = np.cos(angles)[order].T, np.sin(angles)[order].T
    cos_t = np.tile(np.concatenate([cos, cos]), (HEADS, 1)).astype(np.float32)
    sin_t = np.tile(np.concatenate([-sin, sin]), (HEADS, 1)).astype(np.float32)

    arrays = {
        "x": a["L0_attn_a_x"].reshape(BATCH, P, R * D),
        "w_attn": np.stack(w_attn), "b_qk": np.stack(b_qk), "b_v": np.stack(b_v), "b_out": np.stack(b_out),
        "gamma": a["L0_ffn_ln_gamma"].reshape(D, 1), "beta": a["L0_ffn_ln_beta"].reshape(D, 1),
        "fc1_q": a["L0_ffn_fc1_q"], "fc1_s": a["L0_ffn_fc1_scales"].reshape(1, FF),
        "fc1_b": a["L0_ffn_fc1_bias"].reshape(FC, P).T,
        "fc2_q": a["L0_ffn_fc2_q"], "fc2_s": a["L0_ffn_fc2_scales"].reshape(1, FC * D),
        "fc2_b": a["L0_ffn_fc2_bias"].reshape(1, D),
        "cos_t": cos_t, "sin_t": sin_t, "ident_t": np.eye(P, dtype=np.float32),
    }
    arrays = {f"in_{n}": np.ascontiguousarray(v) for n, v in arrays.items()}
    nc = bacc.Bacc("TRN2", target_bir_lowering=False, num_devices=1)
    args = [nc.dram_tensor(n, v.shape, mybir.dt.from_np(v.dtype), kind="ExternalInput").ap() for n, v in arrays.items()]
    args.append(nc.dram_tensor("out_0", (BATCH, P, R * D), F32, kind="ExternalOutput").ap())
    nc.disable_value_cache = True
    hybrid_layers(nc, *args)
    r = run_bass_kernel_spmd(nc, [arrays], core_ids=[0])
    return r.results[0]["out_0"].reshape(BATCH, TOK, D)
```
